# Optimizing a Trainium2 kernel written in Bass

```python
import numpy as np
import jax
import jax.numpy as jnp

def _softmax(x, axis=-1):
    return jax.nn.softmax(x, axis=axis)

def _gelu(x):
    return jax.nn.gelu(x, approximate=True)

def _silu(x):
    return jax.nn.silu(x)

def _sigmoid(x):
    return jax.nn.sigmoid(x)

def _layernorm(x, axis=-1, eps=1e-05):
    m = jnp.mean(x, axis=axis, keepdims=True)
    v = jnp.var(x, axis=axis, keepdims=True)
    return (x - m) / jnp.sqrt(v + eps)

def _scatter_add(tgt, idx, src, axis=0):
    return tgt.at[idx].add(src)

def _segment_sum(src, seg, n):
    return jax.ops.segment_sum(src, seg, n)
kernel_name = 'mk_macaron_d1_jaxref_r8_b9f0d4'

def setup_inputs(seed: int=0):
    np.random.seed(seed)
    _w = jnp.asarray

    def _L0_attn_setup():
        import jax, jax.numpy as jnp
        import numpy as np
        D_MODEL = 128
        NHEAD = 16
        HEAD_DIM = D_MODEL // NHEAD
        LN_EPS = 1e-05

        def _ema_scan(lam, v):
            a = jnp.broadcast_to(lam, v.shape)

            def combine(e1, e2):
                a1, b1 = e1
                a2, b2 = e2
                return (a1 * a2, a2 * b1 + b2)
            _, state = jax.lax.associative_scan(combine, (a, v), axis=1)
            return state
        key = jax.random.key(seed)
        ks = jax.random.split(key, 6)
        B, S = (4, 512)
        x = jax.random.normal(ks[0], (B, S, D_MODEL), dtype=jnp.float32)
        scale = 0.02
        Wq = jax.random.normal(ks[1], (D_MODEL, D_MODEL), dtype=jnp.float32) * scale
        Wv = jax.random.normal(ks[2], (D_MODEL, D_MODEL), dtype=jnp.float32) * scale
        Wo = jax.random.normal(ks[3], (D_MODEL, D_MODEL), dtype=jnp.float32) * scale
        Wg = jax.random.normal(ks[4], (D_MODEL, D_MODEL), dtype=jnp.float32) * scale
        beta = jnp.full((NHEAD,), -0.2, dtype=jnp.float32)
        ln_gamma = jnp.ones((D_MODEL,), dtype=jnp.float32)
        ln_beta = jnp.zeros((D_MODEL,), dtype=jnp.float32)
        return {'x': x, 'Wq': Wq, 'Wv': Wv, 'Wo': Wo, 'Wg': Wg, 'beta': beta, 'ln_gamma': ln_gamma, 'ln_beta': ln_beta}
    _L0_attn_in = _L0_attn_setup()

    def _L0_ffn_setup():
        import jax, jax.numpy as jnp
        import numpy as np
        B, S, H, F, E = (2, 256, 128, 512, 8)
        key = jax.random.key(seed)
        ks = jax.random.split(key, 4)
        x = jax.random.normal(ks[0], (B, S, H), dtype=jnp.float32)
        w_router = jax.random.normal(ks[1], (H, E), dtype=jnp.float32) * 0.02
        w1 = jax.random.normal(ks[2], (E, H, F), dtype=jnp.float32) * 0.02
        b1 = jnp.zeros((E, F), dtype=jnp.float32)
        w2 = jax.random.normal(ks[3], (E, F, H), dtype=jnp.float32) * 0.02
        b2 = jnp.zeros((E, H), dtype=jnp.float32)
        return {'x': x, 'w_router': w_router, 'w1': w1, 'b1': b1, 'w2': w2, 'b2': b2}
    _L0_ffn_in = _L0_ffn_setup()
    _d = {'L0_attn_x': _L0_attn_in['x'], 'L0_attn_Wq': _L0_attn_in['Wq'], 'L0_attn_Wv': _L0_attn_in['Wv'], 'L0_attn_Wo': _L0_attn_in['Wo'], 'L0_attn_Wg': _L0_attn_in['Wg'], 'L0_attn_beta': _L0_attn_in['beta'], 'L0_attn_ln_gamma': _L0_attn_in['ln_gamma'], 'L0_attn_ln_beta': _L0_attn_in['ln_beta'], 'L0_ffn_w_router': _L0_ffn_in['w_router'], 'L0_ffn_w1': _L0_ffn_in['w1'], 'L0_ffn_b1': _L0_ffn_in['b1'], 'L0_ffn_w2': _L0_ffn_in['w2'], 'L0_ffn_b2': _L0_ffn_in['b2']}
    _x0 = _d['L0_attn_x']
    _d['L0_attn_x'] = jax.random.normal(jax.random.fold_in(jax.random.key(seed), 1), (4, 512, 128), dtype=_x0.dtype)
    del _x0
    return _d

def reference(L0_attn_x, L0_attn_Wq, L0_attn_Wv, L0_attn_Wo, L0_attn_Wg, L0_attn_beta, L0_attn_ln_gamma, L0_attn_ln_beta, L0_ffn_w_router, L0_ffn_w1, L0_ffn_b1, L0_ffn_w2, L0_ffn_b2):

    def _L0_attn_ref(x, Wq, Wv, Wo, Wg, beta, ln_gamma, ln_beta):
        import jax, jax.numpy as jnp
        import numpy as np
        D_MODEL = 128
        NHEAD = 16
        HEAD_DIM = D_MODEL // NHEAD
        LN_EPS = 1e-05

        def _ema_scan(lam, v):
            a = jnp.broadcast_to(lam, v.shape)

            def combine(e1, e2):
                a1, b1 = e1
                a2, b2 = e2
                return (a1 * a2, a2 * b1 + b2)
            _, state = jax.lax.associative_scan(combine, (a, v), axis=1)
            return state
        B, S, _ = x.shape
        q = (x @ Wq.T).reshape(B, S, NHEAD, HEAD_DIM)
        v = (x @ Wv.T).reshape(B, S, NHEAD, HEAD_DIM)
        lam = jax.nn.sigmoid(beta).reshape(1, 1, NHEAD, 1).astype(v.dtype)
        state = _ema_scan(lam, v)
        y = (q * state).reshape(B, S, D_MODEL)
        mu = jnp.mean(y, axis=-1, keepdims=True)
        var = jnp.mean(jnp.square(y - mu), axis=-1, keepdims=True)
        y = (y - mu) * jax.lax.rsqrt(var + LN_EPS) * ln_gamma + ln_beta
        gate = jax.nn.silu(x @ Wg.T)
        y = y * gate
        return y @ Wo.T

    def _L0_ffn_ref(x, w_router, w1, b1, w2, b2):
        import jax, jax.numpy as jnp
        import numpy as np
        B, S, H, F, E = (2, 256, 128, 512, 8)
        'Top-1 MoE layer: route -> per-expert FFN -> weighted combine.\n\n            Faithful to ExpertParallelWrapper._process_moe_layer on a single group:\n            router picks one expert per token with a routing weight; tokens are\n            dispatched to experts (here expressed as a static mask over the fixed\n            expert set), processed by the expert FFN, and scatter-combined back\n            weighted by the routing probability.\n            '
        Bs, Ss, Hs = x.shape
        n_experts = w1.shape[0]
        logits = jnp.einsum('bsh,he->bse', x, w_router)
        probs = jax.nn.softmax(logits, axis=-1)
        sel = jnp.argmax(probs, axis=-1)
        wgt = jnp.take_along_axis(probs, sel[..., None], axis=-1)[..., 0]
        xt = x.reshape(-1, Hs)
        sel_t = sel.reshape(-1)
        wgt_t = wgt.reshape(-1)
        out = jnp.zeros_like(xt)
        for e in range(n_experts):
            h = jax.nn.relu(xt @ w1[e] + b1[e])
            y = h @ w2[e] + b2[e]
            m = (sel_t == e).astype(xt.dtype) * wgt_t
            out = out + m[:, None] * y
        return out.reshape(Bs, Ss, Hs)
    x = L0_attn_x
    x = x + 0.5 * _L0_ffn_ref(_layernorm(x, axis=-1), L0_ffn_w_router, L0_ffn_w1, L0_ffn_b1, L0_ffn_w2, L0_ffn_b2)
    x = x + _L0_attn_ref(_layernorm(x, axis=-1), L0_attn_Wq, L0_attn_Wv, L0_attn_Wo, L0_attn_Wg, L0_attn_beta, L0_attn_ln_gamma, L0_attn_ln_beta)
    x = x + 0.5 * _L0_ffn_ref(_layernorm(x, axis=-1), L0_ffn_w_router, L0_ffn_w1, L0_ffn_b1, L0_ffn_w2, L0_ffn_b2)
    return x

_drawn_inputs = setup_inputs


def setup_inputs(seed=0):
    import zlib

    import numpy as np

    out = dict(_drawn_inputs(seed))
    spreads = {'L0_attn_beta': (-0.20000000298023224, 0.6),
     'L0_attn_ln_gamma': (1.0, 0.6),
     'L0_attn_ln_beta': (0.0, 0.8),
     'L0_ffn_b1': (0.0, 0.8),
     'L0_ffn_b2': (0.0, 0.473)}
    factors = {'L0_ffn_w_router': 2.765, 'L0_ffn_w1': 5.335, 'L0_ffn_w2': 4.158}
    for name, (base, spread) in spreads.items():
        noise = np.random.default_rng([zlib.crc32(name.encode()), seed]).standard_normal(out[name].shape)
        drawn = base * np.exp(spread * noise) if base else spread * noise
        out[name] = jnp.asarray(drawn.astype(out[name].dtype))
    for name, factor in factors.items():
        out[name] = (out[name] * factor).astype(out[name].dtype)
    return out
```

```python
from contextlib import ExitStack

import concourse.bass as bass
from concourse import mybir

ALU = mybir.AluOpType
ACT = mybir.ActivationFunctionType
AX_X = mybir.AxisListType.X
F32 = mybir.dt.float32
F16 = mybir.dt.float16
I32 = mybir.dt.int32

P = 128
H = 128
T = 2048
NT = T // P
SEQ = 512
NG = T // SEQ
TG = SEQ // P
E = 8
F = 512
FC = F // P
NJ = NT + E - 1
RING = 4
W1C = F + FC
EPS = 1e-5

C_ID, C_TRI, C_ONE, C_CENTER, C_IOTA, C_DEC, C_MASK, C_TOK = 0, 128, 256, 384, 512, 640, 648, 776
C_END = C_TOK + NT
A_Q, A_V, A_G, A_O, A_GAMMA, A_BETA, A_DECAY, A_ROUTER = 0, 128, 256, 384, 512, 513, 514, 515
A_END = A_ROUTER + E


def program(nc, x, w1, w2, b2, attn, const, out):
    with ExitStack() as ctx:
        def sb(name, shape, dt=F32):
            return ctx.enter_context(nc.sbuf_tensor(name, shape, dt))

        def bank(name):
            return ctx.enter_context(nc.psum_tensor(name, [P, 512], F32))

        def sem(name):
            return ctx.enter_context(nc.semaphore(name))

        def sems(name, n):
            return [sem(f"{name}{i}") for i in range(n)]

        xn_dram = nc.dram_tensor("xn_rows", [T, H], F32, kind="Internal").ap()
        y_dram = nc.dram_tensor("y_slots", [NJ * P, H], F32, kind="Internal").ap()
        xn_rows = xn_dram.rearrange("(p t) h -> p t h", t=NT)
        y_rows = y_dram.rearrange("(j p) h -> p j h", p=P)
        x_rows = x.rearrange("(t p) h -> p t h", p=P)
        out_rows = out.rearrange("(t p) h -> p t h", p=P)

        X = sb("X", [P, NT, H])
        XN = sb("XN", [P, NT, H])
        XNT = sb("XNT", [P, NG, SEQ])
        W1 = sb("W1", [P, E, W1C])
        W2 = sb("W2", [P, E, FC * H])
        B2 = sb("B2", [P, E, H])
        AW = sb("AW", [P, A_END])
        CST = sb("CST", [P, C_END])
        ident = CST[:, C_ID:C_ID + P]

        bns = sb("bns", [P, TG, 6])
        mv = sb("mv", [P, NT, 2])
        vare = sb("vare", [P, NT])
        rstd = sb("rstd", [P, NT])
        neg_half = sb("neg_half", [P, TG])

        rmax = sb("rmax", [P, NT])
        z = sb("z", [P, NT, E])
        ez = sb("ez", [P, NT, E])
        ssum = sb("ssum", [P, NT])
        rsum = sb("rsum", [P, NT])
        prob = sb("prob", [P, NT, E])
        pmax = sb("pmax", [P, NT])
        half_w = sb("half_w", [P, NT])
        key = sb("key", [P, NT, E])
        kmax = sb("kmax", [P, NT])
        oh = sb("oh", [P, E, NT])
        cnt = sb("cnt", [P, E])
        run = sb("run", [P, E, NT])
        tot_i = sb("tot_i", [P, E], I32)
        tiles_i = sb("tiles_i", [P, E], I32)
        tiles_f = sb("tiles_f", [P, E])
        end_t = sb("end_t", [P, E])
        base_t = sb("base_t", [P, E])
        base_s = sb("base_s", [P, E])
        slot_f = sb("slot_f", [P, NT])
        slot_i = sb("slot_i", [P, NT], I32)
        lane_i = sb("lane_i", [P, NT], I32)
        tile_i = sb("tile_i", [P, NT], I32)
        lane_f = sb("lane_f", [P, NT])
        tile_f = sb("tile_f", [P, NT])
        lane_oh = sb("lane_oh", [P, NT, P], F16)
        tile_oh = sb("tile_oh", [P, NT, NJ])
        tile_tok = sb("tile_tok", [P, NT, NJ], F16)
        row_of_slot = sb("row_of_slot", [P, NJ], I32)
        past = sb("past", [P, NJ, E])
        exp_f = sb("exp_f", [P, NJ])
        expert_of_tile = sb("expert_of_tile", [P, NJ], I32)

        xg = sb("xg", [P, RING, H])
        xgt = sb("xgt", [P, 2, P])
        w1c = sb("w1c", [P, 2, W1C])
        hid = sb("hid", [P, 2, F])
        ys = sb("ys", [P, RING, H])
        yt = sb("yt", [P, NT, H])

        decay_t = sb("decay_t", [P, 1])
        decay = sb("decay", [P, 1])
        decay_row = sb("decay_row", [P, SEQ])
        gb_half = sb("gb_half", [P, 2])
        state = sb("state", [P, 2, SEQ])
        yq = sb("yq", [P, 2, SEQ])
        th = sb("th", [P, 2, SEQ])
        gate2 = sb("gate2", [P, 2, SEQ])
        sq = sb("sq", [P, 2, SEQ])
        dg = sb("dg", [P, 2, SEQ])
        bg = sb("bg", [P, 2, SEQ])
        vary = sb("vary", [P, 2, TG])
        rstd_y = sb("rstd_y", [P, 2, TG])

        psT = [bank("psT0"), bank("psT1")]
        psH = [bank("psH0"), bank("psH1")]
        psY = [bank("psY0"), bank("psY1")]
        psR = bank("psR")
        psX = bank("psX")
        psV, psQ, psG, psD = psH[0], psH[1], psY[0], psY[1]

        x_in = sems("x_in", NG)
        w1_in, w2_in, b2_in, aw_in, cst_in = sem("w1_in"), sem("w2_in"), sem("b2_in"), sem("aw_in"), sem("cst_in")
        order = sem("order")
        nh_set = sem("nh_set")
        var_sb, rstd_sb, xn_sb = sems("var_sb", 3), sems("rstd_sb", 3), sems("xn_sb", 3)
        xt_ps, xt_sb = sems("xt_ps", 3), sems("xt_sb", 3)
        logit_ps, z_sb, ez_sb, cnt_sb = sems("logit_ps", 2), sems("z_sb", 2), sems("ez_sb", 2), sems("cnt_sb", 2)
        pref_ps, hot_sb, row_ps, row_sb = sems("pref_ps", 2), sems("hot_sb", 2), sems("row_ps", 2), sems("row_sb", 2)
        exp_sb, xn_out = sems("exp_sb", 2), sems("xn_out", 2)
        xg_in = [sems(f"xg_in{k}_", RING) for k in range(2)]
        y_out = [sems(f"y_out{k}_", RING) for k in range(2)]
        yt_in = [sems(f"yt_in{k}_", NG) for k in range(2)]
        xg_ps, xg_sb, w1_sb, h_ps = sems("xg_ps", 2), sems("xg_sb", 2), sems("w1_sb", 2), sems("h_ps", 2)
        h_sb, y_ps, y_sb = sems("h_sb", 2), sems("y_ps", 2), sems("y_sb", 2)
        dt_sb, decay_sb = sem("dt_sb"), sem("decay_sb")
        v_ps, q_ps, g_ps, scan_sb, yq_sb = sem("v_ps"), sem("q_ps"), sem("g_ps"), sem("scan_sb"), sem("yq_sb")
        d_ps, th_sb, gate_sb, sq_sb, dg_sb, bg_sb = (sem("d_ps"), sem("th_sb"), sem("gate_sb"), sem("sq_sb"),
                                                     sem("dg_sb"), sem("bg_sb"))
        vy_ps, o_ps, vy_sb, ry_sb, x2_sb = sem("vy_ps"), sem("o_ps"), sem("vy_sb"), sem("ry_sb"), sem("x2_sb")
        fin_sb, done = sem("fin_sb"), sem("done")

        def ring_count(j, r):
            return (j - r) * (16 // RING) + 16

        def ring_total(r):
            return 16 * len(range(r, NJ, RING))

        block = ctx.enter_context(nc.Block())

        @block.sync
        def _(sp):
            for g in range(NG):
                sp.dma_start(X[:, g * TG:(g + 1) * TG, :], x_rows[:, g * TG:(g + 1) * TG, :]).then_inc(x_in[g], 16)
                if g == 0:
                    sp.dma_start(CST[:, :], const).then_inc(cst_in, 16)
                    sp.dma_start(AW[:, :], attn).then_inc(aw_in, 16)
            sp.dma_start(W1[:, :, :].rearrange("p e n -> p (e n)"), w1).then_inc(w1_in, 16)
            sp.dma_start(W2[:, :, :].rearrange("p e n -> p (e n)"), w2).then_inc(w2_in, 16)
            sp.dma_start(B2[:, :, :].rearrange("p e n -> p (e n)"), b2.partition_broadcast(P)).then_inc(b2_in, 16)
            for k in range(2):
                for g in range(NG):
                    sp.wait_ge(xn_sb[2 * k], g + 1)
                    sp.dma_start(xn_rows[:, g * TG:(g + 1) * TG, :],
                                 XN[:, g * TG:(g + 1) * TG, :]).then_inc(xn_out[k], 16)

                def store(j, r):
                    sp.wait_ge(y_sb[k], j + 1)
                    sp.dma_start(y_rows[:, bass.ds(j, 1), :].rearrange("p j h -> p (j h)"),
                                 ys[:, r, :]).then_inc(y_out[k][r], 16)

                with sp.Fori(0, NJ // RING) as q:
                    for r in range(RING):
                        store(q * RING + r, r)
                for j in range(NJ - NJ % RING, NJ):
                    store(j, j % RING)
            for g in range(NG):
                sp.wait_ge(fin_sb, g + 1)
                sp.dma_start(out_rows[:, g * TG:(g + 1) * TG, :], X[:, g * TG:(g + 1) * TG, :]).then_inc(done, 16)
            sp.wait_ge(done, 16 * NG)

        @block.gpsimd
        def _(pool):
            nc.gpsimd.memset(neg_half[:, :], -0.5).then_inc(nh_set, 1)
            pool.wait_ge(nh_set, 1)

            def rsqrt_x(n, g):
                c = slice(g * TG, (g + 1) * TG)
                pool.wait_ge(var_sb[n], g + 1)
                nc.gpsimd.tensor_tensor(rstd[:, c], vare[:, c], neg_half[:, :], ALU.pow).then_inc(rstd_sb[n], 1)

            def rsqrt_y(b):
                pool.wait_ge(vy_sb, b + 1)
                nc.gpsimd.tensor_tensor(rstd_y[:, b % 2, :], vary[:, b % 2, :], neg_half[:, :],
                                        ALU.pow).then_inc(ry_sb, 1)

            def gather_slots(k):
                pool.wait_ge(row_sb[k], 1)
                pool.wait_ge(xn_out[k], 16 * NG)
                for j in range(NJ):
                    if j >= RING:
                        pool.wait_ge(xg_ps[k], j - RING + 1)
                    pool.indirect_dma_start(out=xg[:, j % RING, :], out_offset=None, in_=xn_dram,
                                            in_offset=bass.IndirectOffsetOnAxis(ap=row_of_slot[:, j:j + 1], axis=0)
                                            ).then_inc(xg_in[k][j % RING], 16)

            def all_stored(k):
                for r in range(RING):
                    pool.wait_ge(y_out[k][r], ring_total(r))

            def gather_tokens(k, g):
                for t in range(g * TG, (g + 1) * TG):
                    pool.indirect_dma_start(out=yt[:, t, :], out_offset=None, in_=y_dram,
                                            in_offset=bass.IndirectOffsetOnAxis(ap=slot_i[:, t:t + 1], axis=0)
                                            ).then_inc(yt_in[k][g], 16)

            for g in range(NG):
                rsqrt_x(0, g)
            gather_slots(0)
            all_stored(0)
            gather_tokens(0, 0)
            for g in range(1, NG):
                gather_tokens(0, g)
                rsqrt_x(1, g - 1)
            rsqrt_x(1, NG - 1)
            for b in range(NG):
                rsqrt_y(b)
                rsqrt_x(2, b)
            gather_slots(1)
            all_stored(1)
            for g in range(NG):
                gather_tokens(1, g)

        @block.scalar
        def _(act):
            def evacuate(n, g):
                act.wait_ge(xt_ps[n], g + 1)
                nc.scalar.copy(XNT[:, g, :], psT[g % 2][:, :]).then_inc(xt_sb[n], 1)

            def softmax_exp(k):
                act.wait_ge(z_sb[k], 1)
                nc.scalar.activation(ez[:, :, :], z[:, :, :], ACT.Exp).then_inc(ez_sb[k], 1)

            def hidden(k, j, u):
                act.wait_ge(h_ps[k], j + 1)
                act.wait_ge(w1_sb[k], j + 1)
                for c in range(FC):
                    nc.scalar.activation(hid[:, u, c * P:(c + 1) * P], psH[u][:, c * P:(c + 1) * P], ACT.Relu,
                                         bias=w1c[:, u, F + c:F + c + 1]).then_inc(h_sb[k], 1)

            def ffn(k):
                with act.Fori(0, NJ // 2) as q:
                    for u in range(2):
                        hidden(k, q * 2 + u, u)
                for j in range(NJ - NJ % 2, NJ):
                    hidden(k, j, j % 2)

            def tanh_gate(b):
                act.wait_ge(g_ps, b + 1)
                nc.scalar.activation(th[:, b % 2, :], psG[:, :], ACT.Tanh, scale=0.5).then_inc(th_sb, 1)

            def square(b):
                act.wait_ge(d_ps, b + 1)
                nc.scalar.activation(sq[:, b % 2, :], psD[:, :], ACT.Square).then_inc(sq_sb, 1)

            def beta_gate(b):
                act.wait_ge(gate_sb, b + 1)
                nc.scalar.activation(bg[:, b % 2, :], gate2[:, b % 2, :], ACT.Copy,
                                     scale=gb_half[:, 1:2]).then_inc(bg_sb, 1)

            act.wait_ge(aw_in, 16)
            nc.scalar.activation(decay_t[:, :], AW[:, A_DECAY:A_DECAY + 1], ACT.Tanh, scale=0.5).then_inc(dt_sb, 1)
            for g in range(NG):
                evacuate(0, g)
            softmax_exp(0)
            ffn(0)
            act.wait_ge(decay_sb, 1)
            evacuate(1, 0)
            tanh_gate(0)
            evacuate(1, 1)
            for b in range(NG):
                square(b)
                beta_gate(b)
                if b + 1 < NG:
                    tanh_gate(b + 1)
                if b + 2 < NG:
                    evacuate(1, b + 2)
                if b == NG - 2:
                    evacuate(2, 0)
            for g in range(1, NG):
                evacuate(2, g)
            softmax_exp(1)
            ffn(1)

        @block.tensor
        def _(pe):
            def transpose_x(n, g):
                pe.wait_ge(xn_sb[n], g + 1)
                if g >= 2:
                    pe.wait_ge(xt_sb[n], g - 1)
                for i in range(TG):
                    last = nc.tensor.transpose(psT[g % 2][:, i * P:(i + 1) * P], XN[:, g * TG + i, :], ident)
                last.then_inc(xt_ps[n], 1)

            def route(k, g):
                pe.wait_ge(xt_sb[2 * k], g + 1)
                for i in range(TG):
                    t = g * TG + i
                    last = nc.tensor.matmul(psR[:, t * E:(t + 1) * E], XNT[:, g, i * P:(i + 1) * P],
                                            AW[:, A_ROUTER:A_ROUTER + E], start=True, stop=True)
                last.then_inc(logit_ps[k], 1)

            def slot_table(k):
                pe.wait_ge(cnt_sb[k], 1)
                nc.tensor.matmul(psX[:, 0:E], CST[:, C_TRI:C_TRI + P], cnt[:, :], start=True, stop=True)
                nc.tensor.matmul(psX[:, E:2 * E], CST[:, C_ONE:C_ONE + P], cnt[:, :],
                                 start=True, stop=True).then_inc(pref_ps[k], 1)
                pe.wait_ge(hot_sb[k], 1)
                for t in range(NT):
                    last = nc.tensor.matmul(psX[:, 2 * E:2 * E + NJ], lane_oh[:, t, :], tile_tok[:, t, :],
                                            start=(t == 0), stop=(t == NT - 1))
                last.then_inc(row_ps[k], 1)

            def turn(k, j, r):
                pe.wait_ge(xg_in[k][r], ring_count(j, r))
                nc.tensor.transpose(psT[r % 2][:, 0:P], xg[:, r, :], ident).then_inc(xg_ps[k], 1)

            def up(k, j, u):
                pe.wait_ge(xg_sb[k], j + 1)
                for c in range(FC):
                    last = nc.tensor.matmul(psH[u][:, c * P:(c + 1) * P], w1c[:, u, c * P:(c + 1) * P],
                                            xgt[:, u, :], start=True, stop=True)
                last.then_inc(h_ps[k], 1)

            def down(k, j, u, reused):
                if reused:
                    pe.wait_ge(y_sb[k], j - 1)
                e = pe.value_load(expert_of_tile[0:1, bass.ds(j, 1)], min_val=0, max_val=E - 1)
                for c in range(FC):
                    pe.wait_ge(h_sb[k], j * FC + (c + 1))
                    last = nc.tensor.matmul(psY[u][:, 0:H], hid[:, u, c * P:(c + 1) * P],
                                            W2[:, bass.ds(e, 1), c * H:(c + 1) * H].rearrange("p e n -> p (e n)"),
                                            start=(c == 0), stop=(c == FC - 1))
                last.then_inc(y_ps[k], 1)

            def ffn(k):
                pe.wait_ge(exp_sb[k], 1)
                turn(k, 0, 0)
                turn(k, 1, 1)
                up(k, 0, 0)

                def steady(s, r, reused):
                    turn(k, s + 2, (r + 2) % RING)
                    up(k, s + 1, (r + 1) % 2)
                    down(k, s, r % 2, reused)

                for s in range(RING):
                    steady(s, s, s >= 2)
                end = (NJ - 2) - (NJ - 2) % RING
                with pe.Fori(1, end // RING) as q:
                    for r in range(RING):
                        steady(q * RING + r, r, True)
                for s in range(end, NJ - 2):
                    steady(s, s % RING, True)
                up(k, NJ - 1, (NJ - 1) % 2)
                down(k, NJ - 2, (NJ - 2) % 2, True)
                down(k, NJ - 1, (NJ - 1) % 2, True)

            def project(b):
                pe.wait_ge(xt_sb[1], b + 1)
                for bank_, col, sem_, free in ((psV, A_V, v_ps, scan_sb), (psQ, A_Q, q_ps, yq_sb),
                                               (psG, A_G, g_ps, gate_sb)):
                    if b:
                        pe.wait_ge(free, b)
                    nc.tensor.matmul(bank_[:, :], AW[:, col:col + H], XNT[:, b, :],
                                     start=True, stop=True).then_inc(sem_, 1)

            def centre(b):
                pe.wait_ge(yq_sb, b + 1)
                if b:
                    pe.wait_ge(dg_sb, b)
                nc.tensor.matmul(psD[:, :], CST[:, C_CENTER:C_CENTER + P], yq[:, b % 2, :],
                                 start=True, stop=True).then_inc(d_ps, 1)

            def project_out(b):
                pe.wait_ge(sq_sb, b + 1)
                for i in range(TG):
                    last = nc.tensor.matmul(psT[b % 2][:, i:i + 1], sq[:, b % 2, i * P:(i + 1) * P],
                                            CST[:, C_ONE:C_ONE + 1], start=True, stop=True)
                last.then_inc(vy_ps, 1)
                if b:
                    pe.wait_ge(x2_sb, b)
                pe.wait_ge(dg_sb, b + 1)
                for i in range(TG):
                    nc.tensor.matmul(psR[:, i * P:(i + 1) * P], dg[:, b % 2, i * P:(i + 1) * P],
                                     AW[:, A_O:A_O + H], start=True, stop=True)
                pe.wait_ge(bg_sb, b + 1)
                for i in range(TG):
                    last = nc.tensor.matmul(psX[:, i * P:(i + 1) * P], bg[:, b % 2, i * P:(i + 1) * P],
                                            AW[:, A_O:A_O + H], start=True, stop=True)
                last.then_inc(o_ps, 1)

            pe.wait_ge(cst_in, 16)
            pe.wait_ge(aw_in, 16)
            for g in range(NG):
                transpose_x(0, g)
                route(0, g)
            slot_table(0)
            pe.wait_ge(w2_in, 16)
            ffn(0)
            transpose_x(1, 0)
            project(0)
            transpose_x(1, 1)
            for b in range(NG):
                centre(b)
                if b + 1 < NG:
                    project(b + 1)
                project_out(b)
                if b + 2 < NG:
                    pe.wait_ge(vy_sb, b + 1)
                    transpose_x(1, b + 2)
                if b == NG - 2:
                    pe.wait_ge(vy_sb, b + 1)
                    transpose_x(2, 0)
            pe.wait_ge(vy_sb, NG)
            for g in range(1, NG):
                transpose_x(2, g)
            pe.wait_ge(x2_sb, NG)
            for g in range(NG):
                route(1, g)
            slot_table(1)
            ffn(1)

        @block.vector
        def _(dve):
            steps = [0]

            def step(ins):
                steps[0] += 1
                ins.then_inc(order, 1)
                dve.wait_ge(order, steps[0])

            def over(ap, n):
                return ap.unsqueeze(2).broadcast_to([ap.shape[0], ap.shape[1], n])

            def rows(ap, n):
                return ap.unsqueeze(1).broadcast_to([ap.shape[0], n, ap.shape[1]])

            v = nc.vector

            def ln_stats(n, g):
                for i in range(TG):
                    last = v.bn_stats(bns[:, i, :], X[:, g * TG + i, :])
                step(last)
                for i in range(TG):
                    last = v.bn_aggr(mv[:, g * TG + i, :], bns[:, i, :])
                step(last)
                v.tensor_scalar(vare[:, g * TG:(g + 1) * TG], mv[:, g * TG:(g + 1) * TG, 1], EPS, None,
                                ALU.add).then_inc(var_sb[n], 1)

            def ln_apply(n, g):
                dve.wait_ge(rstd_sb[n], g + 1)
                for t in range(g * TG, (g + 1) * TG):
                    last = v.tensor_scalar(XN[:, t, :], X[:, t, :], mv[:, t, 0:1], rstd[:, t:t + 1],
                                           ALU.subtract, ALU.mult)
                last.then_inc(xn_sb[n], 1)

            def routing(k):
                dve.wait_ge(logit_ps[k], NG)
                logits = psR[:, 0:NT * E].rearrange("p (t e) -> p t e", e=E)
                step(v.tensor_reduce(rmax[:, :], logits, AX_X, ALU.max))
                v.tensor_tensor(z[:, :, :], logits, over(rmax[:, :], E), ALU.subtract).then_inc(z_sb[k], 1)
                dve.wait_ge(ez_sb[k], 1)
                step(v.tensor_reduce(ssum[:, :], ez[:, :, :], AX_X, ALU.add))
                step(v.reciprocal(rsum[:, :], ssum[:, :]))
                step(v.tensor_tensor(prob[:, :, :], ez[:, :, :], over(rsum[:, :], E), ALU.mult))
                step(v.tensor_reduce(pmax[:, :], prob[:, :, :], AX_X, ALU.max))
                v.tensor_scalar(half_w[:, :], pmax[:, :], 0.5, None, ALU.mult)
                step(v.tensor_tensor(key[:, :, :], prob[:, :, :], over(pmax[:, :], E), ALU.is_equal))
                step(v.tensor_tensor(key[:, :, :], key[:, :, :], rows(CST[:, C_DEC:C_DEC + E], NT), ALU.mult))
                step(v.tensor_reduce(kmax[:, :], key[:, :, :], AX_X, ALU.max))
                step(v.tensor_tensor(oh[:, :, :].rearrange("p e t -> p t e"), key[:, :, :], over(kmax[:, :], E),
                                     ALU.is_equal))
                v.tensor_reduce(cnt[:, :], oh[:, :, :], AX_X, ALU.add).then_inc(cnt_sb[k], 1)
                step(v.tensor_tensor_scan(run[:, :, :].rearrange("p e t -> p (e t)"), CST[:, C_MASK:C_MASK + NT * E],
                                          oh[:, :, :].rearrange("p e t -> p (e t)"), 0.0, ALU.mult, ALU.add))
                dve.wait_ge(pref_ps[k], 1)
                step(v.tensor_scalar(tot_i[:, :], psX[:, E:2 * E], float(P - 1), None, ALU.add))
                step(v.tensor_scalar(tiles_i[:, :], tot_i[:, :], 7, None, ALU.logical_shift_right))
                step(v.tensor_copy(tiles_f[:, :], tiles_i[:, :]))
                step(v.tensor_tensor_scan(end_t[:, :], CST[:, C_ONE:C_ONE + E], tiles_f[:, :], 0.0,
                                          ALU.mult, ALU.add))
                step(v.tensor_tensor(base_t[:, :], end_t[:, :], tiles_f[:, :], ALU.subtract))
                step(v.scalar_tensor_tensor(base_s[:, :], base_t[:, :], float(P), psX[:, 0:E], ALU.mult, ALU.add))
                step(v.tensor_tensor(run[:, :, :], run[:, :, :], over(base_s[:, :], NT), ALU.add))
                step(v.tensor_tensor(run[:, :, :], run[:, :, :], oh[:, :, :], ALU.mult))
                step(v.tensor_reduce(slot_f[:, :], run[:, :, :].rearrange("p e t -> p t e"), AX_X, ALU.add))
                step(v.tensor_scalar(slot_i[:, :], slot_f[:, :], -1.0, None, ALU.add))
                v.tensor_scalar(lane_i[:, :], slot_i[:, :], P - 1, None, ALU.bitwise_and)
                step(v.tensor_scalar(tile_i[:, :], slot_i[:, :], 7, None, ALU.logical_shift_right))
                v.tensor_copy(lane_f[:, :], lane_i[:, :])
                step(v.tensor_copy(tile_f[:, :], tile_i[:, :]))
                v.tensor_tensor(lane_oh[:, :, :], rows(CST[:, C_IOTA:C_IOTA + P], NT), over(lane_f[:, :], P),
                                ALU.is_equal)
                step(v.tensor_tensor(tile_oh[:, :, :], rows(CST[:, C_IOTA:C_IOTA + NJ], NT), over(tile_f[:, :], NJ),
                                     ALU.is_equal))
                v.tensor_tensor(tile_tok[:, :, :], tile_oh[:, :, :], over(CST[:, C_TOK:C_TOK + NT], NJ),
                                ALU.mult).then_inc(hot_sb[k], 1)
                step(v.tensor_tensor(past[:, :, :], rows(end_t[:, :], NJ), over(CST[:, C_IOTA:C_IOTA + NJ], E),
                                     ALU.is_le))
                step(v.tensor_reduce(exp_f[:, :], past[:, :, :], AX_X, ALU.add))
                v.tensor_scalar(expert_of_tile[:, :], exp_f[:, :], float(E - 1), None, ALU.min).then_inc(exp_sb[k], 1)
                dve.wait_ge(row_ps[k], 1)
                v.tensor_copy(row_of_slot[:, :], psX[:, 2 * E:2 * E + NJ]).then_inc(row_sb[k], 1)

            def expert(j):
                return dve.value_load(expert_of_tile[0:1, bass.ds(j, 1)], min_val=0, max_val=E - 1)

            def fetch(k, j, u):
                e = expert(j)
                v.tensor_copy(w1c[:, u, :], W1[:, bass.ds(e, 1), :].rearrange("p e n -> p (e n)")
                              ).then_inc(w1_sb[k], 1)
                dve.wait_ge(xg_ps[k], j + 1)
                v.tensor_copy(xgt[:, u, :], psT[u][:, 0:P]).then_inc(xg_sb[k], 1)

            def finish(k, j, r, reused):
                e = expert(j)
                if reused:
                    dve.wait_ge(y_out[k][r], ring_count(j, r) - 16)
                dve.wait_ge(y_ps[k], j + 1)
                v.tensor_tensor(ys[:, r, :], psY[r % 2][:, 0:H],
                                B2[:, bass.ds(e, 1), :].rearrange("p e n -> p (e n)"), ALU.add).then_inc(y_sb[k], 1)

            def ffn(k):
                dve.wait_ge(exp_sb[k], 1)
                fetch(k, 0, 0)
                fetch(k, 1, 1)

                def steady(s, r, reused):
                    dve.wait_ge(h_ps[k], s + 1)
                    dve.wait_ge(h_sb[k], FC * s + FC)
                    fetch(k, s + 2, r % 2)
                    finish(k, s, r, reused)

                for s in range(RING):
                    steady(s, s, False)
                end = (NJ - 2) - (NJ - 2) % RING
                with dve.Fori(1, end // RING) as q:
                    for r in range(RING):
                        steady(q * RING + r, r, True)
                for s in range(end, NJ - 2):
                    steady(s, s % RING, True)
                for s in range(NJ - 2, NJ):
                    finish(k, s, s % RING, True)

            def add_ffn(k, g):
                dve.wait_ge(yt_in[k][g], 16 * TG)
                for t in range(g * TG, (g + 1) * TG):
                    last = v.scalar_tensor_tensor(X[:, t, :], yt[:, t, :], half_w[:, t:t + 1], X[:, t, :],
                                                  ALU.mult, ALU.add)
                return last

            def ffn_then_stats(b):
                step(add_ffn(0, b))
                ln_stats(1, b)

            def attend(b):
                u = b % 2
                dve.wait_ge(v_ps, b + 1)
                v.tensor_tensor_scan(state[:, u, :], decay_row[:, :], psV[:, :], 0.0,
                                     ALU.mult, ALU.add).then_inc(scan_sb, 1)
                dve.wait_ge(scan_sb, b + 1)
                dve.wait_ge(q_ps, b + 1)
                v.tensor_tensor(yq[:, u, :], psQ[:, :], state[:, u, :], ALU.mult).then_inc(yq_sb, 1)
                dve.wait_ge(th_sb, b + 1)
                v.scalar_tensor_tensor(gate2[:, u, :], th[:, u, :], 1.0, psG[:, :], ALU.add,
                                       ALU.mult).then_inc(gate_sb, 1)
                dve.wait_ge(gate_sb, b + 1)
                dve.wait_ge(d_ps, b + 1)
                dve.wait_ge(sq_sb, b + 1)
                v.scalar_tensor_tensor(dg[:, u, :], psD[:, :], gb_half[:, 0:1], gate2[:, u, :], ALU.mult,
                                       ALU.mult).then_inc(dg_sb, 1)

            def var_y(b):
                dve.wait_ge(vy_ps, b + 1)
                v.tensor_scalar(vary[:, b % 2, :], psT[b % 2][:, 0:TG], 1.0 / H, EPS, ALU.mult,
                                ALU.add).then_inc(vy_sb, 1)

            def add_attention(b):
                dve.wait_ge(o_ps, b + 1)
                dve.wait_ge(ry_sb, b + 1)
                for i in range(TG):
                    t = b * TG + i
                    last = v.scalar_tensor_tensor(X[:, t, :], psR[:, i * P:(i + 1) * P], rstd_y[:, b % 2, i:i + 1],
                                                  X[:, t, :], ALU.mult, ALU.add)
                step(last)
                chunk = X[:, b * TG:(b + 1) * TG, :].rearrange("p t h -> p (t h)")
                v.tensor_tensor(chunk, chunk, psX[:, :], ALU.add).then_inc(x2_sb, 1)
                dve.wait_ge(x2_sb, b + 1)
                ln_stats(2, b)

            dve.wait_ge(x_in[0], 16)
            ln_stats(0, 0)
            for g in range(1, NG):
                dve.wait_ge(x_in[g], 16)
                ln_stats(0, g)
                ln_apply(0, g - 1)
            ln_apply(0, NG - 1)
            dve.wait_ge(dt_sb, 1)
            v.tensor_scalar(decay[:, :], decay_t[:, :], 0.5, 0.5, ALU.mult, ALU.add)
            v.memset(decay_row[:, :], 1.0)
            step(v.tensor_scalar(gb_half[:, :], AW[:, A_GAMMA:A_GAMMA + 2], 0.5, None, ALU.mult))
            v.tensor_scalar(decay_row[:, :], decay_row[:, :], decay[:, 0:1], None, ALU.mult).then_inc(decay_sb, 1)
            dve.wait_ge(cst_in, 16)
            routing(0)
            dve.wait_ge(w1_in, 16)
            dve.wait_ge(b2_in, 16)
            ffn(0)

            dve.wait_ge(decay_sb, 1)
            ffn_then_stats(0)
            ffn_then_stats(1)
            ln_apply(1, 0)
            ffn_then_stats(2)
            ln_apply(1, 1)
            attend(0)
            ffn_then_stats(3)
            ln_apply(1, 2)
            var_y(0)
            attend(1)
            ln_apply(1, 3)
            add_attention(0)
            var_y(1)
            attend(2)
            add_attention(1)
            ln_apply(2, 0)
            var_y(2)
            attend(3)
            add_attention(2)
            var_y(3)
            ln_apply(2, 1)
            add_attention(3)
            ln_apply(2, 2)
            ln_apply(2, 3)
            routing(1)
            ffn(1)
            for g in range(NG):
                add_ffn(1, g).then_inc(fin_sb, 1)


def kernel(**inputs):
    import numpy as np
    import concourse.bacc as bacc
    from concourse.bass_utils import run_bass_kernel_spmd

    a = {n: np.asarray(v) for n, v in inputs.items()}
    w1 = a["L0_ffn_w1"].transpose(1, 0, 2)
    b1 = a["L0_ffn_b1"].reshape(E, FC, P).transpose(2, 0, 1)
    w2 = a["L0_ffn_w2"].reshape(E, FC, P, H).transpose(2, 0, 1, 3)
    attn = np.concatenate([a["L0_attn_Wq"].T, a["L0_attn_Wv"].T, a["L0_attn_Wg"].T, a["L0_attn_Wo"].T,
                           a["L0_attn_ln_gamma"][:, None], a["L0_attn_ln_beta"][:, None],
                           np.repeat(a["L0_attn_beta"], H // a["L0_attn_beta"].shape[0])[:, None],
                           a["L0_ffn_w_router"]], axis=1)
    const = np.zeros((P, C_END), np.float32)
    const[:, C_ID:C_ID + P] = np.eye(P)
    const[:, C_TRI:C_TRI + P] = np.triu(np.ones((P, P)), 1)
    const[:, C_ONE:C_ONE + P] = 1.0
    const[:, C_CENTER:C_CENTER + P] = np.eye(P) - 1.0 / H
    const[:, C_IOTA:C_IOTA + P] = np.arange(P)
    const[:, C_DEC:C_DEC + E] = E - np.arange(E)
    const[:, C_MASK:C_MASK + NT * E] = np.tile(np.arange(NT) > 0, E)
    const[:, C_TOK:C_TOK + NT] = NT * np.arange(P)[:, None] + np.arange(NT)
    arrays = {
        "x": np.ascontiguousarray(a["L0_attn_x"].reshape(T, H)),
        "w1": np.ascontiguousarray(np.concatenate([w1, b1], axis=2).reshape(P, E * W1C)),
        "w2": np.ascontiguousarray(w2.reshape(P, E * F)),
        "b2": np.ascontiguousarray(a["L0_ffn_b2"].reshape(E * H)),
        "attn": np.ascontiguousarray(attn),
        "const": const,
    }
    nc = bacc.Bacc("TRN2", target_bir_lowering=False, num_devices=1)
    args = [nc.dram_tensor(n, v.shape, mybir.dt.from_np(v.dtype), kind="ExternalInput").ap()
            for n, v in arrays.items()]
    out = nc.dram_tensor("out", (T, H), F32, kind="ExternalOutput").ap()
    program(nc, *args, out)
    r = run_bass_kernel_spmd(nc, [arrays], core_ids=[0])
    return r.results[0]["out"].reshape(a["L0_attn_x"].shape)
```

```python
from contextlib import ExitStack

import concourse.bass as bass
from concourse import mybir

ALU = mybir.AluOpType
ACT = mybir.ActivationFunctionType
AX_X = mybir.AxisListType.X
F32 = mybir.dt.float32
F16 = mybir.dt.float16
I32 = mybir.dt.int32

P = 128
H = 128
T = 2048
NT = T // P
SEQ = 512
NG = T // SEQ
TG = SEQ // P
E = 8
F = 512
FC = F // P
NJ = NT + E - 1
RING = 6
W1C = F + FC
EPS = 1e-5
ROUND = 1.5 * 2.0 ** 23

C_ID, C_TRI, C_ONE, C_CENTER, C_IOTA, C_DEC, C_MASK, C_TOK = 0, 128, 256, 384, 512, 640, 648, 776
C_LANE = C_TOK + NT
C_END = C_LANE + 1
A_Q, A_V, A_G, A_O, A_GAMMA, A_BETA, A_DECAY, A_ROUTER = 0, 128, 256, 384, 512, 513, 514, 515
A_END = A_ROUTER + E


def program(nc, x, w1, w2, b2, attn, const, out):
    with ExitStack() as ctx:
        def sb(name, shape, dt=F32):
            return ctx.enter_context(nc.sbuf_tensor(name, shape, dt))

        def bank(name):
            return ctx.enter_context(nc.psum_tensor(name, [P, 512], F32))

        def sem(name):
            return ctx.enter_context(nc.semaphore(name))

        def sems(name, n):
            return [sem(f"{name}{i}") for i in range(n)]

        xn_dram = nc.dram_tensor("xn_rows", [T + P, H], F32, kind="Internal").ap()
        y_dram = nc.dram_tensor("y_rows", [T, H], F32, kind="Internal").ap()
        xn_rows = xn_dram[0:T, :].rearrange("(p t) h -> p t h", t=NT)
        y_rows = y_dram.rearrange("(p t) h -> p t h", t=NT)
        x_rows = x.rearrange("(t p) h -> p t h", p=P)
        out_rows = out.rearrange("(t p) h -> p t h", p=P)

        X = sb("X", [P, NT, H])
        XN = sb("XN", [P, NT, H])
        XT = sb("XT", [P, NG, SEQ])
        W1 = sb("W1", [P, E, W1C])
        W2 = sb("W2", [P, E, FC * H])
        B2 = sb("B2", [P, E, H])
        AW = sb("AW", [P, A_END])
        CST = sb("CST", [P, C_END])
        ident = CST[:, C_ID:C_ID + P]

        bns = sb("bns", [P, TG, 6])
        mv = sb("mv", [P, NT, 2])
        vare = sb("vare", [P, NT])
        rstd = sb("rstd", [P, NT])
        neg_half = sb("neg_half", [P, TG])

        nmr = sb("nmr", [P, NT])
        nmean = sb("nmean", [P, NT])

        router = sb("router", [P, E])
        logits = sb("logits", [P, NT, E])
        rmax = sb("rmax", [P, NT])
        z = sb("z", [P, NT, E])
        ez = sb("ez", [P, NT, E])
        ssum = sb("ssum", [P, NT])
        prob = sb("prob", [P, NT])
        half_w = sb("half_w", [P, NT])
        key = sb("key", [P, NT, E])
        kmax = sb("kmax", [P, NT])
        oh = sb("oh", [P, E, NT])
        cnt = sb("cnt", [P, E])
        run = sb("run", [P, E, NT])
        part = sb("part", [P, 2 * E, NT])
        tiles_r = sb("tiles_r", [P, E])
        tiles = sb("tiles", [P, 1 + E])
        ends = sb("ends", [P, 1 + E])
        base = sb("base", [P, E])
        slot_f = sb("slot_f", [P, NT])
        slot_i = sb("slot_i", [P, NT], I32)
        lane_i = sb("lane_i", [P, NT], I32)
        tile_i = sb("tile_i", [P, NT], I32)
        lane_oh = sb("lane_oh", [P, NT, P], F16)
        tile_oh = sb("tile_oh", [P, NT, NJ])
        tile_tok = sb("tile_tok", [P, NT, NJ], F16)
        unused = sb("unused", [P, NJ])
        row_of_slot = sb("row_of_slot", [P, NJ], I32)
        past = sb("past", [P, NJ, E])
        exp_f = sb("exp_f", [P, NJ])
        expert_of_tile = sb("expert_of_tile", [P, NJ], I32)

        xg = sb("xg", [P, RING, H])
        xgt = sb("xgt", [P, RING, P])
        w1c = sb("w1c", [P, RING, W1C])
        hid = sb("hid", [P, 2, F])
        ys = sb("ys", [P, RING, H])
        yt = sb("yt", [P, NT, H])

        decay_t = sb("decay_t", [P, 1])
        decay = sb("decay", [P, 1])
        decay_row = sb("decay_row", [P, SEQ])
        gb_half = sb("gb_half", [P, 2])
        state = sb("state", [P, 2, SEQ])
        yq = sb("yq", [P, 2, SEQ])
        th = sb("th", [P, 2, SEQ])
        gate2 = sb("gate2", [P, 2, SEQ])
        sq = sb("sq", [P, 2, SEQ])
        dg = sb("dg", [P, 2, SEQ])
        bg = sb("bg", [P, 2, SEQ])
        vary = sb("vary", [P, 2, TG])
        rstd_y = sb("rstd_y", [P, 2, TG])

        psT = [bank("psT0"), bank("psT1")]
        psH = [bank("psH0"), bank("psH1")]
        psY = [bank("psY0"), bank("psY1")]
        psR = bank("psR")
        psX = bank("psX")
        psV, psQ, psG, psD = psH[0], psH[1], psY[0], psY[1]

        def logit_bank(k, g):
            return (psH + psY)[g] if k == 0 else psT[g % 2]

        x_in = sems("x_in", NG)
        w1_in, w2_in, b2_in, aw_in, cst_in = sem("w1_in"), sem("w2_in"), sem("b2_in"), sem("aw_in"), sem("cst_in")
        order = sem("order")
        nh_set = sem("nh_set")
        var_sb, rstd_sb, xn_sb = sems("var_sb", 3), sems("rstd_sb", 3), sems("xn_sb", 3)
        xt_ps, xt_sb = sems("xt_ps", 3), sems("xt_sb", 3)
        logit_ps, z_sb, ez_sb, cnt_sb = sems("logit_ps", 2), sems("z_sb", 2), sems("ez_sb", 2), sems("cnt_sb", 2)
        pref_ps, hot_sb, row_ps, row_sb = sems("pref_ps", 2), sems("hot_sb", 2), sems("row_ps", 2), sems("row_sb", 2)
        exp_sb, xn_out = sems("exp_sb", 2), sems("xn_out", 2)
        logit_sb = sems("logit_sb", 2)
        pow_sb, spare_out, rw_ps, rw_sb = sem("pow_sb"), sem("spare_out"), sem("rw_ps"), sem("rw_sb")
        xg_in = [sems(f"xg_in{k}_", RING) for k in range(2)]
        y_out = [sems(f"y_out{k}_", RING) for k in range(2)]
        yt_in = [sems(f"yt_in{k}_", NG) for k in range(2)]
        xg_ps, xg_sb, w1_sb, h_ps = sems("xg_ps", 2), sems("xg_sb", 2), sems("w1_sb", 2), sems("h_ps", 2)
        h_sb, y_ps, y_sb = sems("h_sb", 2), sems("y_ps", 2), sems("y_sb", 2)
        dt_sb, decay_sb = sem("dt_sb"), sem("decay_sb")
        v_ps, q_ps, g_ps, scan_sb, yq_sb = sem("v_ps"), sem("q_ps"), sem("g_ps"), sem("scan_sb"), sem("yq_sb")
        d_ps, th_sb, gate_sb, sq_sb, dg_sb, bg_sb = (sem("d_ps"), sem("th_sb"), sem("gate_sb"), sem("sq_sb"),
                                                     sem("dg_sb"), sem("bg_sb"))
        vy_ps, o_ps, vy_sb, ry_sb, x2_sb = sem("vy_ps"), sem("o_ps"), sem("vy_sb"), sem("ry_sb"), sem("x2_sb")
        fin_sb, done = sem("fin_sb"), sem("done")

        def place(q, r):
            return q + r // RING, r % RING

        def ring_total(r):
            return 16 * len(range(r, NJ, RING))

        block = ctx.enter_context(nc.Block())

        @block.sync
        def _(sp):
            for g in range(NG):
                sp.dma_start(X[:, g * TG:(g + 1) * TG, :], x_rows[:, g * TG:(g + 1) * TG, :]).then_inc(x_in[g], 16)
                if g == 0:
                    sp.dma_start(CST[:, :], const).then_inc(cst_in, 16)
                    sp.dma_start(AW[:, :], attn).then_inc(aw_in, 16)
            sp.dma_start(W1[:, :, :].rearrange("p e n -> p (e n)"), w1).then_inc(w1_in, 16)
            sp.dma_start(W2[:, :, :].rearrange("p e n -> p (e n)"), w2).then_inc(w2_in, 16)
            sp.dma_start(B2[:, :, :].rearrange("p e n -> p (e n)"), b2.partition_broadcast(P)).then_inc(b2_in, 16)
            sp.wait_ge(cst_in, 16)
            sp.dma_start(xn_dram[T:T + P, :], ident).then_inc(spare_out, 16)
            for k in range(2):
                for g in range(NG):
                    sp.wait_ge(xn_sb[2 * k], g + 1)
                    sp.dma_start(xn_rows[:, g * TG:(g + 1) * TG, :],
                                 XN[:, g * TG:(g + 1) * TG, :]).then_inc(xn_out[k], 16)
                for r in range(RING):
                    sp.wait_ge(y_out[k][r], ring_total(r))
                for g in range(NG):
                    sp.dma_start(yt[:, g * TG:(g + 1) * TG, :],
                                 y_rows[:, g * TG:(g + 1) * TG, :]).then_inc(yt_in[k][g], 16)
            for g in range(NG):
                sp.wait_ge(fin_sb, g + 1)
                sp.dma_start(out_rows[:, g * TG:(g + 1) * TG, :], X[:, g * TG:(g + 1) * TG, :]).then_inc(done, 16)
            sp.wait_ge(done, 16 * NG)

        @block.gpsimd
        def _(pool):
            nc.gpsimd.memset(neg_half[:, :], -0.5).then_inc(nh_set, 1)
            pool.wait_ge(nh_set, 1)

            def rsqrt_x(n, g):
                c = slice(g * TG, (g + 1) * TG)
                pool.wait_ge(var_sb[n], g + 1)
                nc.gpsimd.tensor_tensor(rstd[:, c], vare[:, c], neg_half[:, :], ALU.pow).then_inc(pow_sb, 1)
                pool.wait_ge(pow_sb, n * NG + g + 1)
                nc.gpsimd.tensor_tensor(nmr[:, c], nmean[:, c], rstd[:, c], ALU.mult).then_inc(rstd_sb[n], 1)

            def rsqrt_y(b):
                pool.wait_ge(vy_sb, b + 1)
                nc.gpsimd.tensor_tensor(rstd_y[:, b % 2, :], vary[:, b % 2, :], neg_half[:, :],
                                        ALU.pow).then_inc(ry_sb, 1)

            def ffn(k):
                pool.wait_ge(row_sb[k], 1)
                pool.wait_ge(xn_out[k], 16 * NG)

                def gather(j):
                    if j >= RING:
                        pool.wait_ge(xg_ps[k], j - RING + 1)
                    pool.indirect_dma_start(out=xg[:, j % RING, :], out_offset=None, in_=xn_dram,
                                            in_offset=bass.IndirectOffsetOnAxis(ap=row_of_slot[:, j:j + 1], axis=0)
                                            ).then_inc(xg_in[k][j % RING], 16)

                for j in range(RING):
                    gather(j)
                for j in range(NJ):
                    pool.wait_ge(y_sb[k], j + 1)
                    pool.indirect_dma_start(out=y_dram, in_=ys[:, j % RING, :], in_offset=None,
                                            out_offset=bass.IndirectOffsetOnAxis(ap=row_of_slot[:, j:j + 1], axis=0),
                                            bounds_check=T - 1, oob_is_err=False).then_inc(y_out[k][j % RING], 16)
                    if j + RING < NJ:
                        gather(j + RING)

            for g in range(NG):
                rsqrt_x(0, g)
            pool.wait_ge(spare_out, 16)
            ffn(0)
            for g in range(NG):
                rsqrt_x(1, g)
            for b in range(NG):
                rsqrt_y(b)
                rsqrt_x(2, b)
            ffn(1)

        @block.scalar
        def _(act):
            def evacuate(n, g):
                act.wait_ge(xt_ps[n], g + 1)
                nc.scalar.copy(XT[:, g, :], psT[g % 2][:, :]).then_inc(xt_sb[n], 1)

            def softmax_exp(k):
                act.wait_ge(z_sb[k], 1)
                nc.scalar.activation(ez[:, :, :], z[:, :, :], ACT.Exp).then_inc(ez_sb[k], 1)

            def normalise(n, g):
                act.wait_ge(rstd_sb[n], g + 1)
                for t in range(g * TG, (g + 1) * TG):
                    last = nc.scalar.activation(XN[:, t, :], X[:, t, :], ACT.Identity, scale=rstd[:, t:t + 1],
                                                bias=nmr[:, t:t + 1])
                last.then_inc(xn_sb[n], 1)

            def hidden(k, j, r):
                u = r % 2
                act.wait_ge(h_ps[k], j + 1)
                act.wait_ge(w1_sb[k], j + 1)
                for c in range(FC):
                    nc.scalar.activation(hid[:, u, c * P:(c + 1) * P], psH[u][:, c * P:(c + 1) * P], ACT.Relu,
                                         bias=w1c[:, r, F + c:F + c + 1]).then_inc(h_sb[k], 1)

            def ffn(k):
                with act.Fori(0, NJ // RING) as q:
                    for r in range(RING):
                        hidden(k, q * RING + r, r)
                for j in range(NJ - NJ % RING, NJ):
                    hidden(k, j, j % RING)

            def tanh_gate(b):
                act.wait_ge(g_ps, b + 1)
                nc.scalar.activation(th[:, b % 2, :], psG[:, :], ACT.Tanh, scale=0.5).then_inc(th_sb, 1)

            def square(b):
                act.wait_ge(d_ps, b + 1)
                nc.scalar.activation(sq[:, b % 2, :], psD[:, :], ACT.Square).then_inc(sq_sb, 1)

            def beta_gate(b):
                act.wait_ge(gate_sb, b + 1)
                nc.scalar.activation(bg[:, b % 2, :], gate2[:, b % 2, :], ACT.Copy,
                                     scale=gb_half[:, 1:2]).then_inc(bg_sb, 1)

            act.wait_ge(aw_in, 16)
            nc.scalar.activation(decay_t[:, :], AW[:, A_DECAY:A_DECAY + 1], ACT.Tanh, scale=0.5).then_inc(dt_sb, 1)
            for g in range(NG):
                evacuate(0, g)
            softmax_exp(0)
            ffn(0)
            act.wait_ge(decay_sb, 1)
            normalise(1, 0)
            evacuate(1, 0)
            normalise(1, 1)
            evacuate(1, 1)
            tanh_gate(0)
            normalise(1, 2)
            square(0)
            beta_gate(0)
            tanh_gate(1)
            evacuate(1, 2)
            normalise(1, 3)
            for b in range(NG):
                if b + 1 < NG:
                    square(b + 1)
                    beta_gate(b + 1)
                if b + 2 < NG:
                    tanh_gate(b + 2)
                evacuate(2, b)
                if b + 3 < NG:
                    evacuate(1, b + 3)
                normalise(2, b)
            softmax_exp(1)
            ffn(1)

        @block.tensor
        def _(pe):
            def transpose_x(n, g, bank_read=None):
                pe.wait_ge(*((x_in[g], 16), (xn_sb[1], g + 1), (x2_sb, g + 1))[n])
                source = XN if n == 1 else X
                if bank_read:
                    pe.wait_ge(*bank_read)
                for i in range(TG):
                    last = nc.tensor.transpose(psT[g % 2][:, i * P:(i + 1) * P], source[:, g * TG + i, :], ident)
                last.then_inc(xt_ps[n], 1)

            def route(k, g):
                pe.wait_ge(xt_sb[2 * k], g + 1)
                for i in range(TG):
                    last = nc.tensor.matmul(logit_bank(k, g)[:, i * E:(i + 1) * E], XT[:, g, i * P:(i + 1) * P],
                                            router[:, :], start=True, stop=True)
                last.then_inc(logit_ps[k], 1)

            def slot_table(k):
                pe.wait_ge(cnt_sb[k], 1)
                nc.tensor.matmul(psX[:, 0:E], CST[:, C_TRI:C_TRI + P], cnt[:, :], start=True, stop=True)
                nc.tensor.matmul(psX[:, E:2 * E], CST[:, C_ONE:C_ONE + P], cnt[:, :],
                                 start=True, stop=True).then_inc(pref_ps[k], 1)
                pe.wait_ge(hot_sb[k], 1)
                for t in range(NT):
                    last = nc.tensor.matmul(psX[:, 2 * E:2 * E + NJ], lane_oh[:, t, :], tile_tok[:, t, :],
                                            start=(t == 0), stop=(t == NT - 1))
                last.then_inc(row_ps[k], 1)

            def turn(k, q, r):
                q, r = place(q, r)
                pe.wait_ge(xg_in[k][r], q * 16 + 16)
                nc.tensor.transpose(psT[r % 2][:, 0:P], xg[:, r, :], ident).then_inc(xg_ps[k], 1)

            def up(k, q, r):
                q, r = place(q, r)
                j, u = q * RING + r, r % 2
                pe.wait_ge(w1_sb[k], j + 1)
                pe.wait_ge(xg_sb[k], j + 1)
                for c in range(FC):
                    last = nc.tensor.matmul(psH[u][:, c * P:(c + 1) * P], w1c[:, r, c * P:(c + 1) * P],
                                            xgt[:, r, :], start=True, stop=True)
                last.then_inc(h_ps[k], 1)

            def down(k, q, r):
                j, u = q * RING + r, r % 2
                if not isinstance(j, int) or j >= 2:
                    pe.wait_ge(y_sb[k], j - 1)
                e = pe.value_load(expert_of_tile[0:1, bass.ds(j, 1)], min_val=0, max_val=E - 1)
                for c in range(FC):
                    pe.wait_ge(h_sb[k], j * FC + (c + 1))
                    last = nc.tensor.matmul(psY[u][:, 0:H], hid[:, u, c * P:(c + 1) * P],
                                            W2[:, bass.ds(e, 1), c * H:(c + 1) * H].rearrange("p e n -> p (e n)"),
                                            start=(c == 0), stop=(c == FC - 1))
                last.then_inc(y_ps[k], 1)

            def ffn(k):
                pe.wait_ge(exp_sb[k], 1)
                turn(k, 0, 0)
                turn(k, 0, 1)
                up(k, 0, 0)

                def steady(q, r):
                    turn(k, q, r + 2)
                    up(k, q, r + 1)
                    down(k, q, r)

                rounds = (NJ - 2) // RING
                for r in range(RING):
                    steady(0, r)
                with pe.Fori(1, rounds) as q:
                    for r in range(RING):
                        steady(q, r)
                for r in range(NJ - 2 - rounds * RING):
                    steady(rounds, r)
                q, r = divmod(NJ - 2, RING)
                up(k, q, r + 1)
                down(k, q, r)
                down(k, *place(q, r + 1))

            def project(b):
                pe.wait_ge(xt_sb[1], b + 1)
                for bank_, col, sem_, free in ((psV, A_V, v_ps, scan_sb), (psQ, A_Q, q_ps, yq_sb),
                                               (psG, A_G, g_ps, gate_sb)):
                    if b:
                        pe.wait_ge(free, b)
                    nc.tensor.matmul(bank_[:, :], AW[:, col:col + H], XT[:, b, :],
                                     start=True, stop=True).then_inc(sem_, 1)

            def centre(b):
                pe.wait_ge(yq_sb, b + 1)
                if b:
                    pe.wait_ge(dg_sb, b)
                nc.tensor.matmul(psD[:, :], CST[:, C_CENTER:C_CENTER + P], yq[:, b % 2, :],
                                 start=True, stop=True).then_inc(d_ps, 1)

            def project_out(b):
                pe.wait_ge(sq_sb, b + 1)
                pe.wait_ge(xt_sb[1], min(b + 3, NG))
                if b >= 2:
                    pe.wait_ge(logit_sb[1], b - 1)
                for i in range(TG):
                    last = nc.tensor.matmul(psT[b % 2][:, i:i + 1], sq[:, b % 2, i * P:(i + 1) * P],
                                            CST[:, C_ONE:C_ONE + 1], start=True, stop=True)
                last.then_inc(vy_ps, 1)
                if b:
                    pe.wait_ge(x2_sb, b)
                pe.wait_ge(dg_sb, b + 1)
                for i in range(TG):
                    nc.tensor.matmul(psR[:, i * P:(i + 1) * P], dg[:, b % 2, i * P:(i + 1) * P],
                                     AW[:, A_O:A_O + H], start=True, stop=True)
                pe.wait_ge(bg_sb, b + 1)
                for i in range(TG):
                    last = nc.tensor.matmul(psX[:, i * P:(i + 1) * P], bg[:, b % 2, i * P:(i + 1) * P],
                                            AW[:, A_O:A_O + H], start=True, stop=True)
                last.then_inc(o_ps, 1)

            pe.wait_ge(cst_in, 16)
            pe.wait_ge(aw_in, 16)
            nc.tensor.matmul(psX[:, 0:E], CST[:, C_CENTER:C_CENTER + P], AW[:, A_ROUTER:A_ROUTER + E],
                             start=True, stop=True).then_inc(rw_ps, 1)
            transpose_x(0, 0)
            transpose_x(0, 1)
            pe.wait_ge(rw_sb, 1)
            for g in range(NG):
                route(0, g)
                if g + 2 < NG:
                    transpose_x(0, g + 2, (xt_sb[0], g + 1))
            slot_table(0)
            pe.wait_ge(w2_in, 16)
            ffn(0)
            transpose_x(1, 0)
            project(0)
            transpose_x(1, 1)
            centre(0)
            project(1)
            transpose_x(1, 2, (xt_sb[1], 1))
            for b in range(NG):
                project_out(b)
                if b + 1 < NG:
                    centre(b + 1)
                if b + 2 < NG:
                    project(b + 2)
                transpose_x(2, b, (vy_sb, b + 1))
                if b + 3 < NG:
                    transpose_x(1, b + 3, (xt_sb[1], b + 2))
                route(1, b)
            slot_table(1)
            ffn(1)

        @block.vector
        def _(dve):
            steps = [0]

            def step(ins):
                steps[0] += 1
                ins.then_inc(order, 1)
                dve.wait_ge(order, steps[0])

            def over(ap, n):
                return ap.unsqueeze(2).broadcast_to([ap.shape[0], ap.shape[1], n])

            def rows(ap, n):
                return ap.unsqueeze(1).broadcast_to([ap.shape[0], n, ap.shape[1]])

            v = nc.vector

            def ln_stats(n, g):
                for i in range(TG):
                    last = v.bn_stats(bns[:, i, :], X[:, g * TG + i, :])
                step(last)
                for i in range(TG):
                    last = v.bn_aggr(mv[:, g * TG + i, :], bns[:, i, :])
                step(last)
                v.tensor_scalar(nmean[:, g * TG:(g + 1) * TG], mv[:, g * TG:(g + 1) * TG, 0], -1.0, None, ALU.mult)
                v.tensor_scalar(vare[:, g * TG:(g + 1) * TG], mv[:, g * TG:(g + 1) * TG, 1], EPS, None,
                                ALU.add).then_inc(var_sb[n], 1)

            def ln_apply(n, g):
                dve.wait_ge(rstd_sb[n], g + 1)
                for t in range(g * TG, (g + 1) * TG):
                    last = v.tensor_scalar(XN[:, t, :], X[:, t, :], mv[:, t, 0:1], rstd[:, t:t + 1],
                                           ALU.subtract, ALU.mult)
                last.then_inc(xn_sb[n], 1)

            def keep_logits(k, g):
                dve.wait_ge(logit_ps[k], g + 1)
                dve.wait_ge(rstd_sb[2 * k], g + 1)
                c = slice(g * TG, (g + 1) * TG)
                v.tensor_tensor(logits[:, c, :], logit_bank(k, g)[:, 0:TG * E].rearrange("p (t e) -> p t e", e=E),
                                over(rstd[:, c], E), ALU.mult).then_inc(logit_sb[k], 1)

            def routing(k):
                dve.wait_ge(logit_sb[k], NG)
                step(v.tensor_reduce(rmax[:, :], logits[:, :, :], AX_X, ALU.max))
                v.tensor_tensor(z[:, :, :], logits[:, :, :], over(rmax[:, :], E), ALU.subtract).then_inc(z_sb[k], 1)
                dve.wait_ge(z_sb[k], 1)
                step(v.scalar_tensor_tensor(key[:, :, :], z[:, :, :], 0.0, rows(CST[:, C_DEC:C_DEC + E], NT),
                                            ALU.is_equal, ALU.mult))
                step(v.tensor_reduce(kmax[:, :], key[:, :, :], AX_X, ALU.max))
                step(v.tensor_tensor(oh[:, :, :].rearrange("p e t -> p t e"), key[:, :, :], over(kmax[:, :], E),
                                     ALU.is_equal))
                v.tensor_reduce(cnt[:, :], oh[:, :, :], AX_X, ALU.add).then_inc(cnt_sb[k], 1)
                step(v.tensor_tensor_scan(run[:, :, :].rearrange("p e t -> p (e t)"), CST[:, C_MASK:C_MASK + NT * E],
                                          oh[:, :, :].rearrange("p e t -> p (e t)"), 0.0, ALU.mult, ALU.add))
                v.tensor_tensor(part[:, 0:E, :], run[:, :, :], oh[:, :, :], ALU.mult)
                dve.wait_ge(pref_ps[k], 1)
                step(v.tensor_scalar(tiles_r[:, :], psX[:, E:2 * E], 0.5 * P - 0.5, 1.0 / P, ALU.add, ALU.mult))
                step(v.tensor_scalar(tiles[:, 1:1 + E], tiles_r[:, :], ROUND, ROUND, ALU.add, ALU.subtract))
                step(v.tensor_tensor_scan(ends[:, :], CST[:, C_ONE:C_ONE + 1 + E], tiles[:, :], -1.0 / P,
                                          ALU.mult, ALU.add))
                step(v.scalar_tensor_tensor(base[:, :], ends[:, 0:E], float(P), psX[:, 0:E], ALU.mult, ALU.add))
                step(v.tensor_tensor(part[:, E:2 * E, :], oh[:, :, :], over(base[:, :], NT), ALU.mult))
                step(v.tensor_reduce(slot_f[:, :], part[:, :, :].rearrange("p e t -> p t e"), AX_X, ALU.add))
                step(v.tensor_copy(slot_i[:, :], slot_f[:, :]))
                v.tensor_scalar(tile_i[:, :], slot_i[:, :], 7, None, ALU.logical_shift_right)
                step(v.tensor_scalar(lane_i[:, :], slot_i[:, :], P - 1, None, ALU.bitwise_and))
                v.tensor_tensor(tile_oh[:, :, :], rows(CST[:, C_IOTA:C_IOTA + NJ], NT), over(tile_i[:, :], NJ),
                                ALU.is_equal)
                step(v.tensor_tensor(lane_oh[:, :, :], rows(CST[:, C_IOTA:C_IOTA + P], NT), over(lane_i[:, :], P),
                                     ALU.is_equal))
                v.tensor_tensor(tile_tok[:, :, :], tile_oh[:, :, :], over(CST[:, C_TOK:C_TOK + NT], NJ),
                                ALU.mult).then_inc(hot_sb[k], 1)
                step(v.tensor_tensor(past[:, :, :], rows(ends[:, 1:1 + E], NJ), over(CST[:, C_IOTA:C_IOTA + NJ], E),
                                     ALU.is_le))
                step(v.tensor_reduce(exp_f[:, :], past[:, :, :], AX_X, ALU.add))
                v.tensor_scalar(expert_of_tile[:, :], exp_f[:, :], float(E - 1), None, ALU.min).then_inc(exp_sb[k], 1)
                dve.wait_ge(row_ps[k], 1)
                step(v.tensor_scalar(unused[:, :], psX[:, 2 * E:2 * E + NJ], 0.0, CST[:, C_LANE:C_LANE + 1],
                                     ALU.is_equal, ALU.mult))
                v.scalar_tensor_tensor(row_of_slot[:, :], psX[:, 2 * E:2 * E + NJ], float(T), unused[:, :],
                                       ALU.add, ALU.add).then_inc(row_sb[k], 1)
                dve.wait_ge(ez_sb[k], 1)
                step(v.tensor_reduce(ssum[:, :], ez[:, :, :], AX_X, ALU.add))
                step(v.reciprocal(prob[:, :], ssum[:, :]))
                step(v.tensor_scalar(half_w[:, :], prob[:, :], 0.5, None, ALU.mult))

            def expert(j):
                return dve.value_load(expert_of_tile[0:1, bass.ds(j, 1)], min_val=0, max_val=E - 1)

            def fetch_w1(k, q, r):
                q, r = place(q, r)
                e = expert(q * RING + r)
                v.tensor_copy(w1c[:, r, :], W1[:, bass.ds(e, 1), :].rearrange("p e n -> p (e n)")
                              ).then_inc(w1_sb[k], 1)

            def fetch_x(k, q, r):
                q, r = place(q, r)
                dve.wait_ge(xg_ps[k], q * RING + (r + 1))
                v.tensor_copy(xgt[:, r, :], psT[r % 2][:, 0:P]).then_inc(xg_sb[k], 1)

            def finish(k, q, r):
                e = expert(q * RING + r)
                if not isinstance(q, int) or q:
                    dve.wait_ge(y_out[k][r], q * 16)
                dve.wait_ge(y_ps[k], q * RING + (r + 1))
                v.tensor_tensor(ys[:, r, :], psY[r % 2][:, 0:H],
                                B2[:, bass.ds(e, 1), :].rearrange("p e n -> p (e n)"), ALU.add).then_inc(y_sb[k], 1)

            def ffn(k):
                dve.wait_ge(exp_sb[k], 1)
                for r in range(3):
                    fetch_w1(k, 0, r)
                fetch_x(k, 0, 0)
                fetch_x(k, 0, 1)

                def steady(q, r):
                    fetch_x(k, q, r + 2)
                    s = q * RING + r
                    if not isinstance(s, int) or s > RING - 3:
                        dve.wait_ge(h_ps[k], s - (RING - 4))
                        dve.wait_ge(h_sb[k], FC * s - FC * (RING - 4))
                    fetch_w1(k, q, r + 3)
                    finish(k, q, r)

                rounds = (NJ - 3) // RING
                for r in range(RING):
                    steady(0, r)
                with dve.Fori(1, rounds) as q:
                    for r in range(RING):
                        steady(q, r)
                for r in range(NJ - 3 - rounds * RING):
                    steady(rounds, r)
                for s in range(NJ - 3, NJ):
                    if s + 2 < NJ:
                        fetch_x(k, *divmod(s + 2, RING))
                    finish(k, *divmod(s, RING))

            def add_ffn(k, g):
                dve.wait_ge(yt_in[k][g], 16)
                for t in range(g * TG, (g + 1) * TG):
                    last = v.scalar_tensor_tensor(X[:, t, :], yt[:, t, :], half_w[:, t:t + 1], X[:, t, :],
                                                  ALU.mult, ALU.add)
                return last

            def ffn_then_stats(b):
                step(add_ffn(0, b))
                ln_stats(1, b)

            def attend(b):
                u = b % 2
                dve.wait_ge(v_ps, b + 1)
                v.tensor_tensor_scan(state[:, u, :], decay_row[:, :], psV[:, :], 0.0,
                                     ALU.mult, ALU.add).then_inc(scan_sb, 1)
                dve.wait_ge(scan_sb, b + 1)
                dve.wait_ge(q_ps, b + 1)
                v.tensor_tensor(yq[:, u, :], psQ[:, :], state[:, u, :], ALU.mult).then_inc(yq_sb, 1)
                dve.wait_ge(th_sb, b + 1)
                v.scalar_tensor_tensor(gate2[:, u, :], th[:, u, :], 1.0, psG[:, :], ALU.add,
                                       ALU.mult).then_inc(gate_sb, 1)

            def gate(b):
                u = b % 2
                dve.wait_ge(gate_sb, b + 1)
                dve.wait_ge(d_ps, b + 1)
                dve.wait_ge(sq_sb, b + 1)
                v.scalar_tensor_tensor(dg[:, u, :], psD[:, :], gb_half[:, 0:1], gate2[:, u, :], ALU.mult,
                                       ALU.mult).then_inc(dg_sb, 1)

            def var_y(b):
                dve.wait_ge(vy_ps, b + 1)
                v.tensor_scalar(vary[:, b % 2, :], psT[b % 2][:, 0:TG], 1.0 / H, EPS, ALU.mult,
                                ALU.add).then_inc(vy_sb, 1)

            def add_attention(b):
                dve.wait_ge(o_ps, b + 1)
                dve.wait_ge(ry_sb, b + 1)
                for i in range(TG):
                    t = b * TG + i
                    last = v.scalar_tensor_tensor(X[:, t, :], psR[:, i * P:(i + 1) * P], rstd_y[:, b % 2, i:i + 1],
                                                  X[:, t, :], ALU.mult, ALU.add)
                step(last)
                chunk = X[:, b * TG:(b + 1) * TG, :].rearrange("p t h -> p (t h)")
                v.tensor_tensor(chunk, chunk, psX[:, :], ALU.add).then_inc(x2_sb, 1)
                dve.wait_ge(x2_sb, b + 1)
                ln_stats(2, b)

            v.memset(tiles[:, 0:1], 0.0)
            for g in range(NG):
                dve.wait_ge(x_in[g], 16)
                ln_stats(0, g)
                if g == 0:
                    dve.wait_ge(rw_ps, 1)
                    v.tensor_copy(router[:, :], psX[:, 0:E]).then_inc(rw_sb, 1)
                if g:
                    ln_apply(0, g - 1)
            ln_apply(0, NG - 1)
            dve.wait_ge(cst_in, 16)
            dve.wait_ge(dt_sb, 1)
            v.tensor_scalar(decay[:, :], decay_t[:, :], 0.5, 0.5, ALU.mult, ALU.add)
            v.memset(decay_row[:, :], 1.0)
            step(v.tensor_scalar(gb_half[:, :], AW[:, A_GAMMA:A_GAMMA + 2], 0.5, None, ALU.mult))
            v.tensor_scalar(decay_row[:, :], decay_row[:, :], decay[:, 0:1], None, ALU.mult).then_inc(decay_sb, 1)
            for g in range(NG):
                keep_logits(0, g)
            routing(0)
            dve.wait_ge(w1_in, 16)
            dve.wait_ge(b2_in, 16)
            ffn(0)

            dve.wait_ge(decay_sb, 1)
            ffn_then_stats(0)
            ffn_then_stats(1)
            attend(0)
            ffn_then_stats(2)
            gate(0)
            ffn_then_stats(3)
            for b in range(NG):
                var_y(b)
                if b + 1 < NG:
                    attend(b + 1)
                add_attention(b)
                if b:
                    keep_logits(1, b - 1)
                if b + 1 < NG:
                    gate(b + 1)
            keep_logits(1, NG - 1)
            routing(1)
            ffn(1)
            for g in range(NG):
                add_ffn(1, g).then_inc(fin_sb, 1)


def kernel(**inputs):
    import numpy as np
    import concourse.bacc as bacc
    from concourse.bass_utils import run_bass_kernel_spmd

    a = {n: np.asarray(v) for n, v in inputs.items()}
    w1 = a["L0_ffn_w1"].transpose(1, 0, 2)
    b1 = a["L0_ffn_b1"].reshape(E, FC, P).transpose(2, 0, 1)
    w2 = a["L0_ffn_w2"].reshape(E, FC, P, H).transpose(2, 0, 1, 3)
    attn = np.concatenate([a["L0_attn_Wq"].T, a["L0_attn_Wv"].T, a["L0_attn_Wg"].T, a["L0_attn_Wo"].T,
                           a["L0_attn_ln_gamma"][:, None], a["L0_attn_ln_beta"][:, None],
                           np.repeat(a["L0_attn_beta"], H // a["L0_attn_beta"].shape[0])[:, None],
                           a["L0_ffn_w_router"]], axis=1)
    const = np.zeros((P, C_END), np.float32)
    const[:, C_ID:C_ID + P] = np.eye(P)
    const[:, C_TRI:C_TRI + P] = np.triu(np.ones((P, P)), 1)
    const[:, C_ONE:C_ONE + P] = 1.0
    const[:, C_CENTER:C_CENTER + P] = np.eye(P) - 1.0 / H
    const[:, C_IOTA:C_IOTA + P] = np.arange(P)
    const[:, C_DEC:C_DEC + E] = E - np.arange(E)
    const[:, C_MASK:C_MASK + NT * E] = np.tile(np.arange(NT) > 0, E)
    const[:, C_TOK:C_TOK + NT] = NT * np.arange(P)[:, None] + np.arange(NT) - T
    const[:, C_LANE] = np.arange(P)
    arrays = {
        "x": np.ascontiguousarray(a["L0_attn_x"].reshape(T, H)),
        "w1": np.ascontiguousarray(np.concatenate([w1, b1], axis=2).reshape(P, E * W1C)),
        "w2": np.ascontiguousarray(w2.reshape(P, E * F)),
        "b2": np.ascontiguousarray(a["L0_ffn_b2"].reshape(E * H)),
        "attn": np.ascontiguousarray(attn),
        "const": const,
    }
    nc = bacc.Bacc("TRN2", target_bir_lowering=False, num_devices=1)
    args = [nc.dram_tensor(n, v.shape, mybir.dt.from_np(v.dtype), kind="ExternalInput").ap()
            for n, v in arrays.items()]
    out = nc.dram_tensor("out", (T, H), F32, kind="ExternalOutput").ap()
    program(nc, *args, out)
    r = run_bass_kernel_spmd(nc, [arrays], core_ids=[0])
    return r.results[0]["out"].reshape(a["L0_attn_x"].shape)
```

```python
from contextlib import ExitStack

import concourse.bass as bass
from concourse import mybir

ALU = mybir.AluOpType
ACT = mybir.ActivationFunctionType
AX_X = mybir.AxisListType.X
F32 = mybir.dt.float32
F16 = mybir.dt.float16
I32 = mybir.dt.int32
I16 = mybir.dt.int16

P = 128
H = 128
T = 2048
NT = T // P
SEQ = 512
NG = T // SEQ
TG = SEQ // P
E = 8
F = 512
FC = F // P
NJ = NT + E - 1
RING = 8
W1C = F + FC
EPS = 1e-5
EARLY = 2
W_SCALE = 4096.0
ROUND = 1.5 * 2.0 ** 23

C_ID, C_TRI, C_ONE, C_CENTER, C_IOTA, C_DEC, C_MASK, C_TOK = 0, 128, 256, 384, 512, 640, 648, 776
C_LANE = C_TOK + NT
C_ROUND = C_LANE + 1
C_SHARE = C_ROUND + 1 + E
C_END = C_SHARE + P
A_Q, A_V, A_G, A_O, A_GAMMA, A_BETA, A_DECAY, A_ROUTER = 0, 128, 256, 384, 512, 513, 514, 515
A_END = A_ROUTER + E


def program(nc, x, w1, w2, b2, attn, const, out):
    with ExitStack() as ctx:
        def sb(name, shape, dt=F32):
            return ctx.enter_context(nc.sbuf_tensor(name, shape, dt))

        def bank(name):
            return ctx.enter_context(nc.psum_tensor(name, [P, 512], F32))

        def sem(name):
            return ctx.enter_context(nc.semaphore(name))

        def sems(name, n):
            return [sem(f"{name}{i}") for i in range(n)]

        xn_dram = nc.dram_tensor("xn_rows", [T + P, H], F32, kind="Internal").ap()
        xn_rows = xn_dram[0:T, :].rearrange("(t p) h -> p t h", p=P)
        x_rows = x.rearrange("(t p) h -> p t h", p=P)
        out_rows = out.rearrange("(t p) h -> p t h", p=P)

        X = sb("X", [P, NT, H])
        XN = sb("XN", [P, NT, H])
        XT = sb("XT", [P, NG, SEQ])
        W1 = sb("W1", [P, E, W1C])
        W2 = sb("W2", [P, E, FC * H])
        B2 = sb("B2", [P, E, H])
        AW = sb("AW", [P, A_END])
        CST = sb("CST", [P, C_END])
        ident = CST[:, C_ID:C_ID + P]

        bns = sb("bns", [P, TG, 6])
        mv = sb("mv", [P, NT, 2])
        vare = sb("vare", [P, NT])
        rstd = sb("rstd", [P, NT])
        neg_half = sb("neg_half", [P, TG])

        nmr = sb("nmr", [P, NT])
        nmean = sb("nmean", [P, NT])

        router = sb("router", [P, E])
        logits = sb("logits", [P, NT, E])
        rmax = sb("rmax", [P, NT])
        z = sb("z", [P, NT, E])
        ez = sb("ez", [P, NT, E])
        ssum = sb("ssum", [P, NT])
        prob = sb("prob", [P, NT])
        half_w = sb("half_w", [P, NT])
        w_parts = sb("w_parts", [P, 3, NT], F16)
        w_rest = sb("w_rest", [P, NT])
        tile_w = sb("tile_w", [P, 3, NJ, NT], F16)
        w_sum = sb("w_sum", [P, NJ])
        w_of_slot = sb("w_of_slot", [P, NJ])
        token_row = sb("token_row", [P, NT], F16)
        key = sb("key", [P, NT, E])
        kmax = sb("kmax", [P, NT])
        oh = sb("oh", [P, E, NT])
        cnt = sb("cnt", [P, E])
        run = sb("run", [P, E, NT])
        part = sb("part", [P, 2 * E, NT])
        tiles = sb("tiles", [P, 1 + E])
        ends = sb("ends", [P, 1 + E])
        base = sb("base", [P, E])
        slot = sb("slot", [P, NT])
        slot_i = sb("slot_i", [P, NT], I16)
        lane_i = sb("lane_i", [P, NT], I16)
        tile_i = sb("tile_i", [P, NT], I16)
        idle = sb("idle", [P, 512], F16)
        iota_h = sb("iota_h", [P, P, NT], I16)
        lane_oh = sb("lane_oh", [P, P, NT], F16)
        tile_oh = sb("tile_oh", [P, NJ, NT], F16)
        tile_tok = sb("tile_tok", [P, NJ, NT], F16)
        unused = sb("unused", [P, NJ])
        row_of_slot = sb("row_of_slot", [P, NJ], I32)
        past = sb("past", [P, NJ, E])
        exp_f = sb("exp_f", [P, NJ])
        expert_of_tile = sb("expert_of_tile", [P, NJ], I32)

        xg = sb("xg", [P, RING, H])
        xgt = sb("xgt", [P, RING, P])
        w1c = sb("w1c", [P, RING, W1C])
        hid = sb("hid", [P, 2, F])
        yb = sb("yb", [P, 2, H])
        ys = sb("ys", [P, RING, H])

        decay_t = sb("decay_t", [P, 1])
        decay = sb("decay", [P, 1])
        decay_row = sb("decay_row", [P, SEQ])
        gb_half = sb("gb_half", [P, 2])
        state = sb("state", [P, 2, SEQ])
        yq = sb("yq", [P, 2, SEQ])
        th = sb("th", [P, 2, SEQ])
        gate2 = sb("gate2", [P, 2, SEQ])
        sq = sb("sq", [P, 2, SEQ])
        dg = sb("dg", [P, 2, SEQ])
        wo_gamma = sb("wo_gamma", [P, H])
        wo_beta = sb("wo_beta", [P, H])
        vary = sb("vary", [P, 2, TG])
        rstd_y = sb("rstd_y", [P, 2, TG])

        psT = [bank("psT0"), bank("psT1")]
        psH = [bank("psH0"), bank("psH1")]
        psY = [bank("psY0"), bank("psY1")]
        psR = bank("psR")
        psX = bank("psX")
        psV, psQ, psG, psD = psH[0], psH[1], psY[0], psY[1]

        def logit_bank(k, g):
            return (psH + psY)[g] if k == 0 else psT[g % 2]

        x_in = sems("x_in", NG)
        w1_in, w2_in, b2_in, aw_in, cst_in = sem("w1_in"), sem("w2_in"), sem("b2_in"), sem("aw_in"), sem("cst_in")
        order = sem("order")
        iota_sb = sem("iota_sb")
        nh_set, idle_sb = sem("nh_set"), sem("idle_sb")
        var_sb, rstd_sb, xn_sb = sems("var_sb", 3), sems("rstd_sb", 3), sems("xn_sb", 3)
        xn1_sb = sems("xn1_sb", NG)
        xt_ps, xt_sb = sems("xt_ps", 3), sems("xt_sb", 3)
        logit_ps, z_sb, ez_sb, cnt_sb = sems("logit_ps", 2), sems("z_sb", 2), sems("ez_sb", 2), sems("cnt_sb", 2)
        pref_ps, hot_sb, row_ps, row_sb = sems("pref_ps", 2), sems("hot_sb", 2), sems("row_ps", 2), sems("row_sb", 2)
        exp_sb, xn_out = sems("exp_sb", 2), sems("xn_out", 2)
        logit_sb = sems("logit_sb", 2)
        pow_sb, spare_out, rw_ps, rw_sb = sem("pow_sb"), sem("spare_out"), sem("rw_ps"), sem("rw_sb")
        xg_in = [sems(f"xg_in{k}_", RING) for k in range(2)]
        y_out = [sems(f"y_out{k}_", RING) for k in range(2)]
        stream_out = sems("stream_out", 2)
        x_back = sems("x_back", NG)
        w_hot, w_ps, b_sb = sems("w_hot", 2), sems("w_ps", 2), sems("b_sb", 2)
        xg_ps, xg_sb, h_ps = sems("xg_ps", 2), sems("xg_sb", 2), sems("h_ps", 2)
        h_sb, y_ps, y_sb = sems("h_sb", 2), sems("y_ps", 2), sems("y_sb", 2)
        dt_sb = sem("dt_sb")
        v_ps, q_ps, g_ps, scan_sb, yq_sb = sem("v_ps"), sem("q_ps"), sem("g_ps"), sem("scan_sb"), sem("yq_sb")
        d_ps, th_sb, gate_sb, sq_sb, dg_sb = sem("d_ps"), sem("th_sb"), sem("gate_sb"), sem("sq_sb"), sem("dg_sb")
        beta_ps = sem("beta_ps")
        vy_ps, o_ps, vy_sb, ry_sb, x2_sb = sem("vy_ps"), sem("o_ps"), sem("vy_sb"), sem("ry_sb"), sem("x2_sb")

        def place(q, r):
            return q + r // RING, r % RING

        def ring_total(r):
            return 16 * len(range(r, NJ, RING))

        block = ctx.enter_context(nc.Block())

        @block.sync
        def _(sp):
            for g in range(NG):
                sp.dma_start(X[:, g * TG:(g + 1) * TG, :], x_rows[:, g * TG:(g + 1) * TG, :]).then_inc(x_in[g], 16)
                if g == 0:
                    sp.dma_start(CST[:, :], const).then_inc(cst_in, 16)
                    sp.dma_start(AW[:, :], attn).then_inc(aw_in, 16)
            sp.dma_start(W1[:, :, :].rearrange("p e n -> p (e n)"), w1).then_inc(w1_in, 16)
            sp.wait_ge(cst_in, 16)
            sp.dma_start(xn_dram[T:T + P, :], ident).then_inc(spare_out, 16)

            def store_xn(k, g):
                sp.wait_ge(xn_sb[2 * k], g + 1)
                sp.dma_start(xn_rows[:, g * TG:(g + 1) * TG, :],
                             XN[:, g * TG:(g + 1) * TG, :]).then_inc(xn_out[k], 16)

            def store_stream(k, g):
                sp.dma_start(out_rows[:, g * TG:(g + 1) * TG, :],
                             X[:, g * TG:(g + 1) * TG, :]).then_inc(stream_out[k], 16)

            for g in range(NG):
                store_xn(0, g)
                if g < EARLY:
                    store_stream(0, g)
            sp.dma_start(W2[:, :, :].rearrange("p e n -> p (e n)"), w2).then_inc(w2_in, 16)
            sp.wait_ge(xg_in[0][0], 16)
            sp.dma_start(B2[:, :, :].rearrange("p e n -> p (e n)"), b2.partition_broadcast(P)).then_inc(b2_in, 16)
            for g in range(EARLY, NG):
                store_stream(0, g)
            for r in range(RING):
                sp.wait_ge(y_out[0][r], ring_total(r))
            for g in range(NG):
                sp.dma_start(X[:, g * TG:(g + 1) * TG, :], out_rows[:, g * TG:(g + 1) * TG, :]).then_inc(x_back[g], 16)
            for g in range(NG):
                sp.wait_ge(x2_sb, g + 1)
                store_stream(1, g)
                store_xn(1, g)
            for r in range(RING):
                sp.wait_ge(y_out[1][r], ring_total(r))

        @block.gpsimd
        def _(pool):
            nc.gpsimd.memset(neg_half[:, :], -0.5).then_inc(nh_set, 1)
            pool.wait_ge(nh_set, 1)

            def rsqrt_x(n, g):
                c = slice(g * TG, (g + 1) * TG)
                pool.wait_ge(var_sb[n], g + 1)
                nc.gpsimd.tensor_tensor(rstd[:, c], vare[:, c], neg_half[:, :], ALU.pow).then_inc(pow_sb, 1)
                pool.wait_ge(pow_sb, n * NG + g + 1)
                nc.gpsimd.tensor_tensor(nmr[:, c], nmean[:, c], rstd[:, c], ALU.mult).then_inc(rstd_sb[n], 1)

            def rsqrt_y(b):
                pool.wait_ge(vy_sb, b + 1)
                nc.gpsimd.tensor_tensor(rstd_y[:, b % 2, :], vary[:, b % 2, :], neg_half[:, :],
                                        ALU.pow).then_inc(ry_sb, 1)

            def ffn(k):
                pool.wait_ge(row_sb[k], 1)
                pool.wait_ge(xn_out[k], 16 * NG)

                def gather(j):
                    if j >= RING:
                        pool.wait_ge(xg_ps[k], j - RING + 1)
                    pool.indirect_dma_start(out=xg[:, j % RING, :], out_offset=None, in_=xn_dram,
                                            in_offset=bass.IndirectOffsetOnAxis(ap=row_of_slot[:, j:j + 1], axis=0)
                                            ).then_inc(xg_in[k][j % RING], 16)

                for j in range(RING):
                    gather(j)
                for j in range(NJ):
                    pool.wait_ge(y_sb[k], j + 1)
                    if j == 0:
                        pool.wait_ge(stream_out[k], 16 * NG)
                    pool.indirect_dma_start(out=out, in_=ys[:, j % RING, :], in_offset=None,
                                            out_offset=bass.IndirectOffsetOnAxis(ap=row_of_slot[:, j:j + 1], axis=0),
                                            bounds_check=T - 1, oob_is_err=False, compute_op=ALU.add
                                            ).then_inc(y_out[k][j % RING], 16)
                    if j + RING < NJ:
                        gather(j + RING)

            for g in range(NG):
                rsqrt_x(0, g)
            pool.wait_ge(spare_out, 16)
            ffn(0)
            for g in range(NG):
                rsqrt_x(1, g)
            for b in range(NG):
                rsqrt_y(b)
                rsqrt_x(2, b)
            ffn(1)

        @block.scalar
        def _(act):
            def evacuate(n, g):
                act.wait_ge(xt_ps[n], g + 1)
                nc.scalar.copy(XT[:, g, :], psT[g % 2][:, :]).then_inc(xt_sb[n], 1)

            def softmax_exp(k):
                act.wait_ge(z_sb[k], 1)
                nc.scalar.activation(ez[:, :, :], z[:, :, :], ACT.Exp).then_inc(ez_sb[k], 1)

            def normalise(n, g, count=TG):
                act.wait_ge(rstd_sb[n], g + 1)
                for t in range(g * TG, g * TG + count):
                    last = nc.scalar.activation(XN[:, t, :], X[:, t, :], ACT.Identity, scale=rstd[:, t:t + 1],
                                                bias=nmr[:, t:t + 1])
                last.then_inc(xn1_sb[g] if n == 1 else xn_sb[n], 1)

            def hidden(k, j, r):
                u = r % 2
                act.wait_ge(h_ps[k], j + 1)
                for c in range(FC):
                    nc.scalar.activation(hid[:, u, c * P:(c + 1) * P], psH[u][:, c * P:(c + 1) * P], ACT.Relu,
                                         bias=w1c[:, r, F + c:F + c + 1]).then_inc(h_sb[k], 1)

            def ffn(k):
                with act.Fori(0, NJ // RING) as q:
                    for r in range(RING):
                        hidden(k, q * RING + r, r)
                for j in range(NJ - NJ % RING, NJ):
                    hidden(k, j, j % RING)

            def tanh_gate(b):
                act.wait_ge(g_ps, b + 1)
                nc.scalar.activation(th[:, b % 2, :], psG[:, :], ACT.Tanh, scale=0.5).then_inc(th_sb, 1)

            def square(b):
                act.wait_ge(d_ps, b + 1)
                nc.scalar.activation(sq[:, b % 2, :], psD[:, :], ACT.Square).then_inc(sq_sb, 1)

            act.wait_ge(cst_in, 16)
            nc.scalar.copy(iota_h[:, :, :], CST[:, C_IOTA:C_IOTA + P].unsqueeze(2).broadcast_to([P, P, NT])
                           ).then_inc(iota_sb, 1)
            act.wait_ge(aw_in, 16)
            nc.scalar.activation(decay_t[:, :], AW[:, A_DECAY:A_DECAY + 1], ACT.Tanh, scale=0.5).then_inc(dt_sb, 1)
            evacuate(0, 0)
            evacuate(0, 1)
            normalise(0, 0)
            evacuate(0, 2)
            evacuate(0, 3)
            normalise(0, 1)
            normalise(0, 2)
            softmax_exp(0)
            normalise(0, 3)
            ffn(0)
            normalise(1, 0, TG // 2)
            evacuate(1, 0)
            evacuate(1, 1)
            tanh_gate(0)
            square(0)
            normalise(1, 3)
            tanh_gate(1)
            evacuate(1, 2)
            for b in range(NG):
                if b + 1 < NG:
                    square(b + 1)
                if b + 2 < NG:
                    tanh_gate(b + 2)
                evacuate(2, b)
                if b + 3 < NG:
                    evacuate(1, b + 3)
                normalise(2, b)
            softmax_exp(1)
            ffn(1)

        @block.tensor
        def _(pe):
            def keep_warm(n, bank_):
                for _ in range(n):
                    nc.tensor.matmul(bank_[:, :], idle[:, 0:P], idle[:, :], start=True, stop=True)

            def transpose_x(n, g, bank_read=None):
                pe.wait_ge(*((x_in[g], 16), (xn1_sb[g], 1 if g else 2), (x2_sb, g + 1))[n])
                source = XN if n == 1 else X
                if bank_read:
                    pe.wait_ge(*bank_read)
                for i in range(TG):
                    last = nc.tensor.transpose(psT[g % 2][:, i * P:(i + 1) * P], source[:, g * TG + i, :], ident)
                last.then_inc(xt_ps[n], 1)

            def route(k, g):
                pe.wait_ge(xt_sb[2 * k], g + 1)
                for i in range(TG):
                    last = nc.tensor.matmul(logit_bank(k, g)[:, i * E:(i + 1) * E], XT[:, g, i * P:(i + 1) * P],
                                            router[:, :], start=True, stop=True)
                last.then_inc(logit_ps[k], 1)

            def slot_table(k):
                keep_warm(6, psR)
                pe.wait_ge(cnt_sb[k], 1)
                nc.tensor.matmul(psX[:, 0:E], CST[:, C_TRI:C_TRI + P], cnt[:, :], start=True, stop=True)
                nc.tensor.matmul(psX[:, E:2 * E], CST[:, C_SHARE:C_SHARE + P], cnt[:, :],
                                 start=True, stop=True).then_inc(pref_ps[k], 1)
                keep_warm(7, psR)
                pe.wait_ge(hot_sb[k], 1)
                for t in range(NT):
                    last = nc.tensor.matmul(psX[:, 2 * E:2 * E + NJ], lane_oh[:, :, t], tile_tok[:, :, t],
                                            start=(t == 0), stop=(t == NT - 1))
                last.then_inc(row_ps[k], 1)

            def slot_weights(k):
                pe.wait_ge(w_hot[k], 1)
                for t in range(NT):
                    last = nc.tensor.matmul(psR[:, 0:3 * NJ], lane_oh[:, :, t],
                                            tile_w[:, :, :, t].rearrange("p a j -> p (a j)"),
                                            start=(t == 0), stop=(t == NT - 1))
                last.then_inc(w_ps[k], 1)

            def turn(k, q, r):
                q, r = place(q, r)
                pe.wait_ge(xg_in[k][r], q * 16 + 16)
                nc.tensor.transpose(psT[r % 2][:, 0:P], xg[:, r, :], ident).then_inc(xg_ps[k], 1)

            def up(k, q, r):
                q, r = place(q, r)
                j, u = q * RING + r, r % 2
                pe.wait_ge(xg_sb[k], j + 1)
                for c in range(FC):
                    last = nc.tensor.matmul(psH[u][:, c * P:(c + 1) * P], w1c[:, r, c * P:(c + 1) * P],
                                            xgt[:, r, :], start=True, stop=True)
                last.then_inc(h_ps[k], 1)

            def down(k, q, r):
                j, u = q * RING + r, r % 2
                e = pe.value_load(expert_of_tile[0:1, bass.ds(j, 1)], min_val=0, max_val=E - 1)
                for c in range(FC):
                    pe.wait_ge(h_sb[k], j * FC + (c + 1))
                    last = nc.tensor.matmul(psY[u][:, 0:H], hid[:, u, c * P:(c + 1) * P],
                                            W2[:, bass.ds(e, 1), c * H:(c + 1) * H].rearrange("p e n -> p (e n)"),
                                            start=(c == 0), stop=(c == FC - 1))
                last.then_inc(y_ps[k], 1)

            def ffn(k):
                keep_warm(12, psH[0])
                slot_weights(k)
                pe.wait_ge(exp_sb[k], 1)
                turn(k, 0, 0)
                turn(k, 0, 1)
                up(k, 0, 0)

                def steady(q, r):
                    turn(k, q, r + 2)
                    up(k, q, r + 1)
                    if k == 0 and isinstance(q, int) and q + r == 0:
                        pe.wait_ge(w2_in, 16)
                    down(k, q, r)

                steady(0, 0)
                steady(0, 1)
                rounds = (NJ - 4) // RING
                with pe.Fori(0, rounds) as q:
                    for r in range(2, 2 + RING):
                        steady(q, r)
                for j in range(2 + rounds * RING, NJ - 2):
                    steady(*divmod(j, RING))
                q, r = divmod(NJ - 2, RING)
                up(k, q, r + 1)
                down(k, q, r)
                pe.wait_ge(b_sb[k], NJ - 2)
                down(k, *place(q, r + 1))

            def project(b):
                pe.wait_ge(xt_sb[1], b + 1)
                for bank_, col, sem_, free in ((psV, A_V, v_ps, scan_sb), (psQ, A_Q, q_ps, yq_sb),
                                               (psG, A_G, g_ps, gate_sb)):
                    if b:
                        pe.wait_ge(free, b)
                    nc.tensor.matmul(bank_[:, :], AW[:, col:col + H], XT[:, b, :],
                                     start=True, stop=True).then_inc(sem_, 1)

            def centre(b):
                pe.wait_ge(yq_sb, b + 1)
                if b:
                    pe.wait_ge(dg_sb, b)
                nc.tensor.matmul(psD[:, :], CST[:, C_CENTER:C_CENTER + P], yq[:, b % 2, :],
                                 start=True, stop=True).then_inc(d_ps, 1)

            def token_variance(b):
                pe.wait_ge(sq_sb, b + 1)
                pe.wait_ge(xt_sb[1], min(b + 3, NG) if b else 1)
                if b >= 2:
                    pe.wait_ge(logit_sb[1], b - 1)
                for i in range(TG):
                    last = nc.tensor.matmul(psT[b % 2][:, i:i + 1], sq[:, b % 2, i * P:(i + 1) * P],
                                            CST[:, C_ONE:C_ONE + 1], start=True, stop=True)
                last.then_inc(vy_ps, 1)

            def out_beta(b):
                pe.wait_ge(gate_sb, b + 1)
                if b:
                    pe.wait_ge(x2_sb, b)
                for i in range(TG):
                    last = nc.tensor.matmul(psX[:, i * P:(i + 1) * P], gate2[:, b % 2, i * P:(i + 1) * P],
                                            wo_beta[:, :], start=True, stop=True)
                last.then_inc(beta_ps, 1)

            def out_gamma(b):
                pe.wait_ge(dg_sb, b + 1)
                for i in range(TG):
                    last = nc.tensor.matmul(psR[:, i * P:(i + 1) * P], dg[:, b % 2, i * P:(i + 1) * P],
                                            wo_gamma[:, :], start=True, stop=True)
                last.then_inc(o_ps, 1)

            pe.wait_ge(idle_sb, 1)
            keep_warm(10, psR)
            pe.wait_ge(cst_in, 16)
            pe.wait_ge(aw_in, 16)
            nc.tensor.matmul(psX[:, 0:E], CST[:, C_CENTER:C_CENTER + P], AW[:, A_ROUTER:A_ROUTER + E],
                             start=True, stop=True).then_inc(rw_ps, 1)
            transpose_x(0, 0)
            transpose_x(0, 1)
            pe.wait_ge(rw_sb, 1)
            for g in range(NG):
                route(0, g)
                if g + 2 < NG:
                    transpose_x(0, g + 2, (xt_sb[0], g + 1))
            slot_table(0)
            ffn(0)
            keep_warm(20, psR)
            pe.wait_ge(x_back[0], 16)
            keep_warm(12, psR)
            transpose_x(1, 0)
            keep_warm(2, psR)
            project(0)
            transpose_x(1, 1)
            centre(0)
            project(1)
            out_beta(0)
            token_variance(0)
            out_gamma(0)
            transpose_x(1, 2, (vy_sb, 1))
            for b in range(NG):
                if b + 1 < NG:
                    centre(b + 1)
                if b + 2 < NG:
                    project(b + 2)
                elif b + 2 == NG:
                    keep_warm(4, psQ)
                if b + 1 == NG:
                    keep_warm(7, psV)
                transpose_x(2, b, (vy_sb, b + 1))
                if b + 3 < NG:
                    transpose_x(1, b + 3, (xt_sb[1], b + 2))
                if b + 1 < NG:
                    out_beta(b + 1)
                else:
                    keep_warm(5, psV)
                if b + 1 < NG:
                    token_variance(b + 1)
                    out_gamma(b + 1)
                route(1, b)
            slot_table(1)
            ffn(1)

        @block.vector
        def _(dve):
            steps = [0]

            def mark(ins):
                steps[0] += 1
                ins.then_inc(order, 1)
                return steps[0]

            def step(ins):
                dve.wait_ge(order, mark(ins))

            def over(ap, n):
                return ap.unsqueeze(2).broadcast_to([ap.shape[0], ap.shape[1], n])

            def rows(ap, n):
                return ap.unsqueeze(1).broadcast_to([ap.shape[0], n, ap.shape[1]])

            v = nc.vector

            def ln_stats(n, g):
                for i in range(TG):
                    last = v.bn_stats(bns[:, i, :], X[:, g * TG + i, :])
                step(last)
                for i in range(TG):
                    last = v.bn_aggr(mv[:, g * TG + i, :], bns[:, i, :])
                step(last)
                v.tensor_scalar(nmean[:, g * TG:(g + 1) * TG], mv[:, g * TG:(g + 1) * TG, 0], -1.0, None, ALU.mult)
                v.tensor_scalar(vare[:, g * TG:(g + 1) * TG], mv[:, g * TG:(g + 1) * TG, 1], EPS, None,
                                ALU.add).then_inc(var_sb[n], 1)

            def keep_logits(k, g):
                dve.wait_ge(logit_ps[k], g + 1)
                dve.wait_ge(rstd_sb[2 * k], g + 1)
                c = slice(g * TG, (g + 1) * TG)
                v.tensor_tensor(logits[:, c, :], logit_bank(k, g)[:, 0:TG * E].rearrange("p (t e) -> p t e", e=E),
                                over(rstd[:, c], E), ALU.mult).then_inc(logit_sb[k], 1)

            def routing(k):
                dve.wait_ge(logit_sb[k], NG)
                step(v.tensor_reduce(rmax[:, :], logits[:, :, :], AX_X, ALU.max))
                v.tensor_tensor(z[:, :, :], logits[:, :, :], over(rmax[:, :], E), ALU.subtract).then_inc(z_sb[k], 1)
                dve.wait_ge(z_sb[k], 1)
                step(v.scalar_tensor_tensor(key[:, :, :], z[:, :, :], 0.0, rows(CST[:, C_DEC:C_DEC + E], NT),
                                            ALU.is_equal, ALU.mult))
                step(v.tensor_reduce(kmax[:, :], key[:, :, :], AX_X, ALU.max))
                step(v.tensor_tensor(oh[:, :, :].rearrange("p e t -> p t e"), key[:, :, :], over(kmax[:, :], E),
                                     ALU.is_equal))
                v.tensor_reduce(cnt[:, :], oh[:, :, :], AX_X, ALU.add).then_inc(cnt_sb[k], 1)
                counted = mark(v.tensor_tensor_scan(run[:, :, :].rearrange("p e t -> p (e t)"),
                                                    CST[:, C_MASK:C_MASK + NT * E],
                                                    oh[:, :, :].rearrange("p e t -> p (e t)"), 0.0, ALU.mult, ALU.add))
                dve.wait_ge(ez_sb[k], 1)
                summed = mark(v.tensor_reduce(ssum[:, :], ez[:, :, :], AX_X, ALU.add))
                dve.wait_ge(order, counted)
                v.tensor_tensor(part[:, 0:E, :], run[:, :, :], oh[:, :, :], ALU.mult)
                dve.wait_ge(order, summed)
                inverted = mark(v.reciprocal(prob[:, :], ssum[:, :]))
                dve.wait_ge(pref_ps[k], 1)
                rounded = mark(v.tensor_scalar(tiles[:, 1:1 + E], psX[:, E:2 * E], 0.5 - 0.5 / P, ROUND,
                                               ALU.add, ALU.add))
                dve.wait_ge(order, inverted)
                weighted = mark(v.tensor_scalar(half_w[:, :], prob[:, :], 0.5 * W_SCALE, None, ALU.mult))
                dve.wait_ge(order, rounded)
                added = mark(v.tensor_tensor_scan(ends[:, :], CST[:, C_ROUND:C_ROUND + 1 + E], tiles[:, :], 0.0,
                                                  ALU.add, ALU.add))
                dve.wait_ge(order, weighted)
                first = mark(v.tensor_copy(w_parts[:, 0, :], half_w[:, :]))
                dve.wait_ge(order, added)
                based = mark(v.scalar_tensor_tensor(base[:, :], ends[:, 0:E], float(P), psX[:, 0:E], ALU.mult, ALU.add))
                dve.wait_ge(order, first)
                rest = mark(v.tensor_tensor(w_rest[:, :], half_w[:, :], w_parts[:, 0, :], ALU.subtract))
                dve.wait_ge(order, based)
                placed = mark(v.tensor_tensor(part[:, E:2 * E, :], oh[:, :, :], over(base[:, :], NT), ALU.mult))
                dve.wait_ge(order, rest)
                second = mark(v.tensor_copy(w_parts[:, 1, :], w_rest[:, :]))
                dve.wait_ge(order, placed)
                slotted = mark(v.tensor_reduce(slot[:, :], part[:, :, :].rearrange("p e t -> p t e"), AX_X, ALU.add))
                dve.wait_ge(order, second)
                v.tensor_tensor(w_parts[:, 2, :], w_rest[:, :], w_parts[:, 1, :], ALU.subtract)
                dve.wait_ge(order, slotted)
                step(v.tensor_scalar(slot_i[:, :], slot[:, :], -1.0, None, ALU.add))
                v.tensor_scalar(tile_i[:, :], slot_i[:, :], 7, None, ALU.logical_shift_right)
                step(v.tensor_scalar(lane_i[:, :], slot_i[:, :], P - 1, None, ALU.bitwise_and))
                hot = mark(v.tensor_tensor(tile_oh[:, :, :], iota_h[:, 0:NJ, :], rows(tile_i[:, :], NJ), ALU.is_equal))
                v.tensor_tensor(lane_oh[:, :, :], iota_h[:, :, :], rows(lane_i[:, :], P), ALU.is_equal)
                dve.wait_ge(order, hot)
                v.tensor_tensor(tile_tok[:, :, :], tile_oh[:, :, :], rows(token_row[:, :], NJ),
                                ALU.mult).then_inc(hot_sb[k], 1)
                step(v.tensor_tensor(past[:, :, :], rows(ends[:, 1:1 + E], NJ), over(CST[:, C_IOTA:C_IOTA + NJ], E),
                                     ALU.is_le))
                counted = mark(v.tensor_reduce(exp_f[:, :], past[:, :, :], AX_X, ALU.add))
                dve.wait_ge(row_ps[k], 1)
                step(v.tensor_scalar(unused[:, :], psX[:, 2 * E:2 * E + NJ], 0.0, CST[:, C_LANE:C_LANE + 1],
                                     ALU.is_equal, ALU.mult))
                v.scalar_tensor_tensor(row_of_slot[:, :], psX[:, 2 * E:2 * E + NJ], float(T), unused[:, :],
                                       ALU.add, ALU.add).then_inc(row_sb[k], 1)
                dve.wait_ge(order, counted)
                v.tensor_scalar(expert_of_tile[:, :], exp_f[:, :], float(E - 1), None, ALU.min).then_inc(exp_sb[k], 1)

            def expert(j):
                return dve.value_load(expert_of_tile[0:1, bass.ds(j, 1)], min_val=0, max_val=E - 1)

            def fetch_w1(k, q, r):
                q, r = place(q, r)
                e = expert(q * RING + r)
                v.tensor_copy(w1c[:, r, :], W1[:, bass.ds(e, 1), :].rearrange("p e n -> p (e n)"))

            def fetch_x(k, q, r):
                q, r = place(q, r)
                dve.wait_ge(xg_ps[k], q * RING + (r + 1))
                v.tensor_copy(xgt[:, r, :], psT[r % 2][:, 0:P]).then_inc(xg_sb[k], 1)

            def finish(k, q, r):
                e = expert(q * RING + r)
                if q:
                    dve.wait_ge(y_out[k][r], q * 16)
                elif k + r == 0:
                    dve.wait_ge(b2_in, 16)
                dve.wait_ge(y_ps[k], q * RING + (r + 1))
                v.tensor_tensor(yb[:, r % 2, :], psY[r % 2][:, 0:H],
                                B2[:, bass.ds(e, 1), :].rearrange("p e n -> p (e n)"), ALU.add).then_inc(b_sb[k], 1)
                dve.wait_ge(b_sb[k], q * RING + (r + 1))
                weight = w_of_slot[:, bass.ds(q * RING + r, 1)]
                v.tensor_tensor(ys[:, r, :], yb[:, r % 2, :], weight.broadcast_to([P, H]),
                                ALU.mult).then_inc(y_sb[k], 1)

            def ffn(k):
                dve.wait_ge(exp_sb[k], 1)
                for r in range(3):
                    fetch_w1(k, 0, r)
                for a in range(3):
                    last = v.tensor_tensor(tile_w[:, a, :, :], tile_oh[:, :, :], rows(w_parts[:, a, :], NJ), ALU.mult)
                last.then_inc(w_hot[k], 1)
                fetch_x(k, 0, 0)
                fetch_x(k, 0, 1)
                dve.wait_ge(w_ps[k], 1)
                step(v.tensor_reduce(w_sum[:, :], psR[:, 0:3 * NJ].rearrange("p (a j) -> p j a", a=3), AX_X, ALU.add))
                step(v.tensor_scalar(w_of_slot[:, :], w_sum[:, :], 1.0 / W_SCALE, None, ALU.mult))

                def steady(q, r):
                    fetch_x(k, q, r + 2)
                    fetch_w1(k, q, r + 3)
                    finish(k, q, r)

                for j in range(NJ - 3):
                    steady(*divmod(j, RING))
                for s in range(NJ - 3, NJ):
                    if s + 2 < NJ:
                        fetch_x(k, *divmod(s + 2, RING))
                    finish(k, *divmod(s, RING))

            def stream_stats(b):
                dve.wait_ge(x_back[b], 16)
                ln_stats(1, b)

            def normalise(g, start=0):
                dve.wait_ge(rstd_sb[1], g + 1)
                for t in range(g * TG + start, (g + 1) * TG):
                    last = v.tensor_scalar(XN[:, t, :], X[:, t, :], mv[:, t, 0:1], rstd[:, t:t + 1],
                                           ALU.subtract, ALU.mult)
                last.then_inc(xn1_sb[g], 1)

            def attend(b):
                u = b % 2
                dve.wait_ge(v_ps, b + 1)
                v.tensor_tensor_scan(state[:, u, :], decay_row[:, :], psV[:, :], 0.0,
                                     ALU.mult, ALU.add).then_inc(scan_sb, 1)
                dve.wait_ge(scan_sb, b + 1)
                dve.wait_ge(q_ps, b + 1)
                v.tensor_tensor(yq[:, u, :], psQ[:, :], state[:, u, :], ALU.mult).then_inc(yq_sb, 1)
                dve.wait_ge(th_sb, b + 1)
                v.scalar_tensor_tensor(gate2[:, u, :], th[:, u, :], 1.0, psG[:, :], ALU.add,
                                       ALU.mult).then_inc(gate_sb, 1)

            def gate(b):
                u = b % 2
                dve.wait_ge(gate_sb, b + 1)
                dve.wait_ge(d_ps, b + 1)
                dve.wait_ge(sq_sb, b + 1)
                v.tensor_tensor(dg[:, u, :], psD[:, :], gate2[:, u, :], ALU.mult).then_inc(dg_sb, 1)

            def var_y(b):
                dve.wait_ge(vy_ps, b + 1)
                v.tensor_scalar(vary[:, b % 2, :], psT[b % 2][:, 0:TG], 1.0 / H, EPS, ALU.mult,
                                ALU.add).then_inc(vy_sb, 1)

            def add_attention(b):
                dve.wait_ge(o_ps, b + 1)
                dve.wait_ge(beta_ps, b + 1)
                dve.wait_ge(ry_sb, b + 1)
                for i in range(TG):
                    t = b * TG + i
                    last = v.scalar_tensor_tensor(X[:, t, :], psR[:, i * P:(i + 1) * P], rstd_y[:, b % 2, i:i + 1],
                                                  X[:, t, :], ALU.mult, ALU.add)
                step(last)
                chunk = X[:, b * TG:(b + 1) * TG, :].rearrange("p t h -> p (t h)")
                v.tensor_tensor(chunk, chunk, psX[:, :], ALU.add).then_inc(x2_sb, 1)
                dve.wait_ge(x2_sb, b + 1)
                ln_stats(2, b)

            v.memset(idle[:, :], 0.0).then_inc(idle_sb, 1)
            v.memset(tiles[:, 0:1], ROUND)
            for g in range(NG):
                dve.wait_ge(x_in[g], 16)
                ln_stats(0, g)
                if g == 0:
                    dve.wait_ge(rw_ps, 1)
                    v.tensor_copy(router[:, :], psX[:, 0:E]).then_inc(rw_sb, 1)
            dve.wait_ge(cst_in, 16)
            v.tensor_copy(token_row[:, :], CST[:, C_TOK:C_TOK + NT])
            dve.wait_ge(iota_sb, 1)
            for g in range(NG):
                keep_logits(0, g)
            routing(0)
            dve.wait_ge(w1_in, 16)
            ffn(0)

            dve.wait_ge(dt_sb, 1)
            v.tensor_scalar(decay[:, :], decay_t[:, :], 0.5, 0.5, ALU.mult, ALU.add)
            v.memset(decay_row[:, :], 1.0)
            step(v.tensor_scalar(gb_half[:, :], AW[:, A_GAMMA:A_GAMMA + 2], 0.5, None, ALU.mult))
            v.tensor_scalar(decay_row[:, :], decay_row[:, :], decay[:, 0:1], None, ALU.mult)
            v.tensor_scalar(wo_gamma[:, :], AW[:, A_O:A_O + H], gb_half[:, 0:1], None, ALU.mult)
            step(v.tensor_scalar(wo_beta[:, :], AW[:, A_O:A_O + H], gb_half[:, 1:2], None, ALU.mult))
            stream_stats(0)
            stream_stats(1)
            normalise(0, TG // 2)
            stream_stats(2)
            normalise(1)
            stream_stats(3)
            attend(0)
            gate(0)
            normalise(2)
            for b in range(NG):
                var_y(b)
                if b + 1 < NG:
                    attend(b + 1)
                add_attention(b)
                if b:
                    keep_logits(1, b - 1)
                if b + 1 < NG:
                    gate(b + 1)
            keep_logits(1, NG - 1)
            routing(1)
            ffn(1)


def kernel(**inputs):
    import numpy as np
    import concourse.bacc as bacc
    from concourse.bass_utils import run_bass_kernel_spmd

    a = {n: np.asarray(v) for n, v in inputs.items()}
    w1 = a["L0_ffn_w1"].transpose(1, 0, 2)
    b1 = a["L0_ffn_b1"].reshape(E, FC, P).transpose(2, 0, 1)
    w2 = a["L0_ffn_w2"].reshape(E, FC, P, H).transpose(2, 0, 1, 3)
    attn = np.concatenate([a["L0_attn_Wq"].T, a["L0_attn_Wv"].T, a["L0_attn_Wg"].T, a["L0_attn_Wo"].T,
                           a["L0_attn_ln_gamma"][:, None], a["L0_attn_ln_beta"][:, None],
                           np.repeat(a["L0_attn_beta"], H // a["L0_attn_beta"].shape[0])[:, None],
                           a["L0_ffn_w_router"]], axis=1)
    const = np.zeros((P, C_END), np.float32)
    const[:, C_ID:C_ID + P] = np.eye(P)
    const[:, C_TRI:C_TRI + P] = np.triu(np.ones((P, P)), 1)
    const[:, C_ONE:C_ONE + P] = 1.0
    const[:, C_CENTER:C_CENTER + P] = np.eye(P) - 1.0 / H
    const[:, C_IOTA:C_IOTA + P] = np.arange(P)
    const[:, C_DEC:C_DEC + E] = E - np.arange(E)
    const[:, C_MASK:C_MASK + NT * E] = np.tile(np.arange(NT) > 0, E)
    const[:, C_TOK:C_TOK + NT] = np.arange(P)[:, None] + P * np.arange(NT) - T
    const[:, C_LANE] = np.arange(P)
    const[:, C_ROUND:C_ROUND + 1 + E] = -ROUND
    const[:, C_SHARE:C_SHARE + P] = 1.0 / P
    arrays = {
        "x": np.ascontiguousarray(a["L0_attn_x"].reshape(T, H)),
        "w1": np.ascontiguousarray(np.concatenate([w1, b1], axis=2).reshape(P, E * W1C)),
        "w2": np.ascontiguousarray(w2.reshape(P, E * F)),
        "b2": np.ascontiguousarray(a["L0_ffn_b2"].reshape(E * H)),
        "attn": np.ascontiguousarray(attn),
        "const": const,
    }
    nc = bacc.Bacc("TRN2", target_bir_lowering=False, num_devices=1)
    args = [nc.dram_tensor(n, v.shape, mybir.dt.from_np(v.dtype), kind="ExternalInput").ap()
            for n, v in arrays.items()]
    out = nc.dram_tensor("out", (T, H), F32, kind="ExternalOutput").ap()
    program(nc, *args, out)
    r = run_bass_kernel_spmd(nc, [arrays], core_ids=[0])
    return r.results[0]["out"].reshape(a["L0_attn_x"].shape)
```
